# Optimizing a Trainium2 kernel written in Bass

```python
import numpy as np
import jax
import jax.numpy as jnp

def _softmax(x, axis=-1):
    return jax.nn.softmax(x, axis=axis)

def _gelu(x):
    return jax.nn.gelu(x, approximate=True)

def _silu(x):
    return jax.nn.silu(x)

def _sigmoid(x):
    return jax.nn.sigmoid(x)

def _layernorm(x, axis=-1, eps=1e-05):
    m = jnp.mean(x, axis=axis, keepdims=True)
    v = jnp.var(x, axis=axis, keepdims=True)
    return (x - m) / jnp.sqrt(v + eps)

def _scatter_add(tgt, idx, src, axis=0):
    return tgt.at[idx].add(src)

def _segment_sum(src, seg, n):
    return jax.ops.segment_sum(src, seg, n)
kernel_name = 'mk_cond_resid_d4_seqx_r8_7f0c8b'

def setup_inputs(seed: int=0):
    np.random.seed(seed)
    _w = jnp.asarray

    def _rec_inputs():
        import jax
        import jax.numpy as jnp
        _rk = jax.random.key(seed)
        x = -7.109e-05 + 0.9999 * jax.random.normal(jax.random.fold_in(_rk, 1), (32, 32, 256), jnp.float32)
        _lenS = 32 - jax.random.randint(jax.random.fold_in(_rk, 7), (32,), 0, max(1, 32 // 4) + 1, jnp.int32)
        _lenS2 = 32 - jax.random.randint(jax.random.fold_in(_rk, 8), (32,), 0, max(1, 32 // 4) + 1, jnp.int32)
        itok_B_0_7 = jax.random.randint(jax.random.fold_in(_rk, 11), (32,), 0, 8, jnp.int32)
        itok_Bx257_0_4111 = jax.random.randint(jax.random.fold_in(_rk, 12), (32, 257), 0, 514, jnp.int32)
        itok_B_37_3939 = jax.random.randint(jax.random.fold_in(_rk, 13), (32,), 37, 3940, jnp.int32)
        itok_B_1_198 = jax.random.randint(jax.random.fold_in(_rk, 14), (32,), 1, 199, jnp.int32)
        itok_B_0_6 = jax.random.randint(jax.random.fold_in(_rk, 15), (32,), 0, 7, jnp.int32)
        return (x, itok_B_0_7, itok_Bx257_0_4111, itok_B_37_3939, itok_B_1_198, itok_B_0_6)
    x, itok_B_0_7, itok_Bx257_0_4111, itok_B_37_3939, itok_B_1_198, itok_B_0_6 = _rec_inputs()

    def _L0_cond_setup():
        import jax, jax.numpy as jnp
        import numpy as np
        B, C, D, T, N_SUBJECTS = (128, 32, 32, 256, 8)
        key = jax.random.key(seed)
        kx, ks, kw = jax.random.split(key, 3)
        x = jax.random.normal(kx, (B, C, T), dtype=jnp.float32)
        subjects = jax.random.randint(ks, (B,), 0, N_SUBJECTS, dtype=jnp.int64)
        weights = jax.random.normal(kw, (N_SUBJECTS, C, D), dtype=jnp.float32) * (1.0 / C ** 0.5)
        return {'x': x, 'subjects': subjects, 'weights': weights}
    _L0_cond_all = _L0_cond_setup()
    _L0_cond_in = {k: v for k, v in _L0_cond_all.items() if k in ('weights',)}
    del _L0_cond_all

    def _L1_cond_setup():
        import jax, jax.numpy as jnp
        import numpy as np
        H, G, HD = (8, 4, 32)
        GSZ = H // G
        BLOCK = 16
        WINDOW = 128
        SCALE = 256.0 ** (-0.5)
        EPS = 1e-06
        THETA = 10000.0
        B, T, D = (16, 4, 256)
        NBLK = 257

        def _rms(x, scale):
            var = jnp.mean(x * x, axis=-1, keepdims=True)
            return x * jax.lax.rsqrt(var + EPS) * (1.0 + scale)

        def _rope(x, pos):
            half = HD // 2
            inv = 1.0 / THETA ** (jnp.arange(half, dtype=jnp.float32) / half)
            ang = pos[:, :, None].astype(jnp.float32) * inv
            cos = jnp.cos(ang)[:, None, :, :]
            sin = jnp.sin(ang)[:, None, :, :]
            x1, x2 = (x[..., :half], x[..., half:])
            return jnp.concatenate([x1 * cos - x2 * sin, x2 * cos + x1 * sin], axis=-1)
        key = jax.random.key(seed)
        ks = jax.random.split(key, 10)
        inv_d = 1.0 / np.sqrt(D)
        return {'x': jax.random.normal(ks[0], (B, T, D), jnp.float32), 'Wq': jax.random.normal(ks[1], (H * HD, D), jnp.float32) * inv_d, 'Wk': jax.random.normal(ks[2], (G * HD, D), jnp.float32) * inv_d, 'Wv': jax.random.normal(ks[3], (G * HD, D), jnp.float32) * inv_d, 'Wo': jax.random.normal(ks[4], (D, H * HD), jnp.float32) * inv_d, 'q_norm_scale': jax.random.normal(ks[5], (HD,), jnp.float32) * 0.02, 'k_norm_scale': jax.random.normal(ks[6], (HD,), jnp.float32) * 0.02, 'k_blocks': jax.random.normal(ks[7], (B * NBLK, G, BLOCK, HD), jnp.float32), 'v_blocks': jax.random.normal(ks[8], (B * NBLK, G, BLOCK, HD), jnp.float32), 'block_tables': jnp.arange(B * NBLK, dtype=jnp.int32).reshape(B, NBLK), 'kv_lens': jax.random.randint(ks[9], (B,), 0, 512, dtype=jnp.int32)}
    _L1_cond_all = _L1_cond_setup()
    _L1_cond_in = {k: v for k, v in _L1_cond_all.items() if k in ('Wq', 'Wk', 'Wv', 'Wo', 'q_norm_scale', 'k_norm_scale', 'k_blocks', 'v_blocks')}
    del _L1_cond_all

    def _L2_cond_setup():
        import jax, jax.numpy as jnp
        import numpy as np
        B, C, T = (128, 32, 256)
        S, D = (200, 32)
        key = jax.random.key(seed)
        k1, k2, k3 = jax.random.split(key, 3)
        x = jax.random.normal(k1, (B, C, T), dtype=jnp.float32)
        conditions = jax.random.randint(k2, (B,), 0, S, dtype=jnp.int64)
        weights = jax.random.normal(k3, (S, C, D), dtype=jnp.float32) / jnp.sqrt(jnp.float32(C))
        return {'x': x, 'conditions': conditions, 'weights': weights}
    _L2_cond_all = _L2_cond_setup()
    _L2_cond_in = {k: v for k, v in _L2_cond_all.items() if k in ('weights',)}
    del _L2_cond_all

    def _L3_cond_setup():
        import jax, jax.numpy as jnp
        import numpy as np
        B, T, D_IN, D_OUT = (16, 256, 256, 256)
        N_ADAPTERS, RANK = (8, 16)
        key = jax.random.key(seed)
        k_x, k_w, k_a, k_b, k_s, k_idx = jax.random.split(key, 6)
        x = jax.random.normal(k_x, (B, T, D_IN), dtype=jnp.float32)
        W = jax.random.normal(k_w, (D_OUT, D_IN), dtype=jnp.float32) * (1.0 / np.sqrt(D_IN))
        A = jax.random.normal(k_a, (N_ADAPTERS, RANK, D_IN), dtype=jnp.float32) * 0.02
        Bm = jax.random.normal(k_b, (N_ADAPTERS, D_OUT, RANK), dtype=jnp.float32) * 0.02
        scalings = jnp.ones((N_ADAPTERS,), dtype=jnp.float32)
        adapter_idx = jax.random.randint(k_idx, (B,), 0, N_ADAPTERS, dtype=jnp.int32)
        return {'x': x, 'W': W, 'A': A, 'Bm': Bm, 'scalings': scalings, 'adapter_idx': adapter_idx}
    _L3_cond_all = _L3_cond_setup()
    _L3_cond_in = {k: v for k, v in _L3_cond_all.items() if k in ('W', 'A', 'Bm', 'scalings')}
    del _L3_cond_all
    return {'x': x, 'itok_B_0_7': itok_B_0_7, 'itok_Bx257_0_4111': itok_Bx257_0_4111, 'itok_B_37_3939': itok_B_37_3939, 'itok_B_1_198': itok_B_1_198, 'itok_B_0_6': itok_B_0_6, 'L0_cond_weights': _L0_cond_in['weights'], 'L1_cond_Wq': _L1_cond_in['Wq'], 'L1_cond_Wk': _L1_cond_in['Wk'], 'L1_cond_Wv': _L1_cond_in['Wv'], 'L1_cond_Wo': _L1_cond_in['Wo'], 'L1_cond_q_norm_scale': _L1_cond_in['q_norm_scale'], 'L1_cond_k_norm_scale': _L1_cond_in['k_norm_scale'], 'L1_cond_k_blocks': _L1_cond_in['k_blocks'], 'L1_cond_v_blocks': _L1_cond_in['v_blocks'], 'L2_cond_weights': _L2_cond_in['weights'], 'L3_cond_W': _L3_cond_in['W'], 'L3_cond_A': _L3_cond_in['A'], 'L3_cond_Bm': _L3_cond_in['Bm'], 'L3_cond_scalings': _L3_cond_in['scalings']}

def reference(x, itok_B_0_7, itok_Bx257_0_4111, itok_B_37_3939, itok_B_1_198, itok_B_0_6, L0_cond_weights, L1_cond_Wq, L1_cond_Wk, L1_cond_Wv, L1_cond_Wo, L1_cond_q_norm_scale, L1_cond_k_norm_scale, L1_cond_k_blocks, L1_cond_v_blocks, L2_cond_weights, L3_cond_W, L3_cond_A, L3_cond_Bm, L3_cond_scalings):
    import jax
    import jax.numpy as jnp

    def _L0_cond_ref(x, subjects, weights):
        import jax, jax.numpy as jnp
        import numpy as np
        B, C, D, T, N_SUBJECTS = (128, 32, 32, 256, 8)
        w = weights[subjects]
        out = jnp.einsum('bct,bcd->bdt', x, w)
        return out

    def _L1_cond_ref(x, Wq, Wk, Wv, Wo, q_norm_scale, k_norm_scale, k_blocks, v_blocks, block_tables, kv_lens):
        import jax, jax.numpy as jnp
        import numpy as np
        H, G, HD = (8, 4, 32)
        GSZ = H // G
        BLOCK = 16
        WINDOW = 128
        SCALE = 256.0 ** (-0.5)
        EPS = 1e-06
        THETA = 10000.0
        B, T, D = (16, 4, 256)
        NBLK = 257

        def _rms(x, scale):
            var = jnp.mean(x * x, axis=-1, keepdims=True)
            return x * jax.lax.rsqrt(var + EPS) * (1.0 + scale)

        def _rope(x, pos):
            half = HD // 2
            inv = 1.0 / THETA ** (jnp.arange(half, dtype=jnp.float32) / half)
            ang = pos[:, :, None].astype(jnp.float32) * inv
            cos = jnp.cos(ang)[:, None, :, :]
            sin = jnp.sin(ang)[:, None, :, :]
            x1, x2 = (x[..., :half], x[..., half:])
            return jnp.concatenate([x1 * cos - x2 * sin, x2 * cos + x1 * sin], axis=-1)
        Bx, Tx, _ = x.shape
        q = jnp.einsum('btd,od->bto', x, Wq).reshape(Bx, Tx, H, HD).transpose(0, 2, 1, 3)
        k = jnp.einsum('btd,od->bto', x, Wk).reshape(Bx, Tx, G, HD).transpose(0, 2, 1, 3)
        v = jnp.einsum('btd,od->bto', x, Wv).reshape(Bx, Tx, G, HD).transpose(0, 2, 1, 3)
        q = _rms(q, q_norm_scale)
        k = _rms(k, k_norm_scale)
        pos = kv_lens[:, None] + jnp.arange(Tx, dtype=jnp.int32)
        q = _rope(q, pos)
        k = _rope(k, pos)
        slot = pos // BLOCK
        off = pos % BLOCK
        blk = jnp.take_along_axis(block_tables, slot, axis=1)
        k_blocks = k_blocks.at[blk, :, off, :].set(k.transpose(0, 2, 1, 3))
        v_blocks = v_blocks.at[blk, :, off, :].set(v.transpose(0, 2, 1, 3))
        k_all = k_blocks[block_tables].transpose(0, 2, 1, 3, 4).reshape(Bx, G, -1, HD)
        v_all = v_blocks[block_tables].transpose(0, 2, 1, 3, 4).reshape(Bx, G, -1, HD)
        S = k_all.shape[2]
        qg = q.reshape(Bx, G, GSZ, Tx, HD)
        scores = jnp.einsum('bghtd,bgsd->bghts', qg, k_all) * SCALE
        kpos = jnp.arange(S, dtype=jnp.int32)
        allowed = (kpos[None, None, :] <= pos[:, :, None]) & (kpos[None, None, :] > pos[:, :, None] - WINDOW)
        scores = jnp.where(allowed[:, None, None, :, :], scores, -jnp.inf)
        p = jax.nn.softmax(scores, axis=-1)
        o = jnp.einsum('bghts,bgsd->bghtd', p, v_all).reshape(Bx, H, Tx, HD)
        o = o.transpose(0, 2, 1, 3).reshape(Bx, Tx, H * HD)
        return jnp.einsum('bto,do->btd', o, Wo)

    def _L2_cond_ref(x, conditions, weights):
        import jax, jax.numpy as jnp
        import numpy as np
        B, C, T = (128, 32, 256)
        S, D = (200, 32)
        w = weights[conditions]
        return jnp.einsum('bct,bcd->bdt', x, w)

    def _L3_cond_ref(x, W, A, Bm, scalings, adapter_idx):
        import jax, jax.numpy as jnp
        import numpy as np
        B, T, D_IN, D_OUT = (16, 256, 256, 256)
        N_ADAPTERS, RANK = (8, 16)
        H = jnp.einsum('btd,od->bto', x, W)
        A_b = A[adapter_idx]
        B_b = Bm[adapter_idx]
        s_b = scalings[adapter_idx]
        xa = jnp.einsum('btd,brd->btr', x, A_b)
        delta = jnp.einsum('btr,bor->bto', xa, B_b)
        delta = jax.lax.stop_gradient(delta * s_b[:, None, None])
        return H + delta
    x = x + _L0_cond_ref(x, itok_B_0_7, L0_cond_weights)
    x = x + _L1_cond_ref(x, L1_cond_Wq, L1_cond_Wk, L1_cond_Wv, L1_cond_Wo, L1_cond_q_norm_scale, L1_cond_k_norm_scale, L1_cond_k_blocks, L1_cond_v_blocks, itok_Bx257_0_4111, itok_B_37_3939)
    x = x + _L2_cond_ref(x, itok_B_1_198, L2_cond_weights)
    x = x + _L3_cond_ref(x, L3_cond_W, L3_cond_A, L3_cond_Bm, L3_cond_scalings, itok_B_0_6)
    return x

_drawn_inputs = setup_inputs


def setup_inputs(seed=0):
    import zlib

    import numpy as np

    out = dict(_drawn_inputs(seed))
    spreads = {'L3_cond_scalings': (1.0, 0.6)}
    factors = {'L1_cond_Wk': 13.489,
     'L1_cond_q_norm_scale': 26.67,
     'L1_cond_k_norm_scale': 64.0,
     'L1_cond_k_blocks': 2.929,
     'L3_cond_A': 3.067,
     'L3_cond_Bm': 3.045}
    for name, (base, spread) in spreads.items():
        noise = np.random.default_rng([zlib.crc32(name.encode()), seed]).standard_normal(out[name].shape)
        drawn = base * np.exp(spread * noise) if base else spread * noise
        out[name] = jnp.asarray(drawn.astype(out[name].dtype))
    for name, factor in factors.items():
        out[name] = (out[name] * factor).astype(out[name].dtype)
    return out
```

```python
import concourse.bass as bass
from concourse import mybir
from contextlib import ExitStack

F32 = mybir.dt.float32
I32 = mybir.dt.int32
U32 = mybir.dt.uint32
ALU = mybir.AluOpType
ACT = mybir.ActivationFunctionType
AX_X = mybir.AxisListType.X

P = 128
B, T, D = 32, 32, 256
G, HPG, HD = 4, 2, 32
H = G * HPG
BLOCK, NBLK, NPHYS = 16, 257, 4112
WINDOW = 128
SCALE = 256.0 ** -0.5
EPS = 1e-6
NT = B * T // P
BPT = P // T
NS = WINDOW // BLOCK + 3
NW = 3
SP_ = NS * BLOCK
HP = SP_ // 2
NU = NW * B
NG = 3
GR = [128, 128, NU]
KVW = 2 * G * HD
BIG = 1e30
PI = 3.1415925
TWO_PI = (6.28125, 0.0019350051879882812, 3.019916050561733e-07)
MAGIC = 12582912.0

_C = [("ident", 128), ("bdmask", 128), ("u1", NU), ("k16", NU), ("b32", NU), ("rel", SP_), ("invf", 16),
      ("s8", NG), ("b257", 1), ("t", 1), ("t128", 1), ("j1", NT), ("btok", NT), ("aid", 1), ("halfpi", 1),
      ("eps", 1)]
C_AT, NC_ = {}, 0
for _n, _w in _C:
    C_AT[_n] = (NC_, _w)
    NC_ += _w
_I = [("kvtok", NT), ("kvrow", 1), ("kvb", B), ("subj", NT), ("cond", NT), ("adapt", B)]
I_AT, NI_ = {}, 0
for _n, _w in _I:
    I_AT[_n] = (NI_, _w)
    NI_ += _w
NPOS = NT + 1 + B


def program(nc, x, ints, consts, fdata, table, kv, w0, w2, wqkv, wo, w3, ball, out):
    kv_new = nc.dram_tensor("kv_new", (NU, BLOCK * KVW), F32, kind="Internal").ap()
    x_rows = x.rearrange("(i p) f -> p i f", p=P)
    out_rows = out.rearrange("(i p) f -> p i f", p=P)

    ctx = ExitStack()
    with ctx:
        def sb(name, shape, dt=F32):
            return ctx.enter_context(nc.sbuf_tensor(name, shape, dt))

        def pb(name, shape, dt=F32):
            return ctx.enter_context(nc.psum_tensor(name, shape, dt))

        def sem(name):
            return ctx.enter_context(nc.semaphore(name))

        cst = sb("cst", [P, NC_])
        ii = sb("ii", [P, NI_], I32)
        fd = sb("fd", [P, 65])
        xs = sb("xs", [P, NT, D])
        wqkv_sb = sb("wqkv_sb", [P, 2, 512])
        wo_sb = sb("wo_sb", [P, HPG, D])
        w3_sb = sb("w3_sb", [P, 2, 384])
        ball_sb = sb("ball_sb", [P, D])
        win = sb("win", [P, NG, BLOCK * KVW])
        KT = sb("KT", [P, B, NS, BLOCK])
        VT = sb("VT", [P, B, NS, BLOCK])
        scratch = VT[:, :, :, :].rearrange("p b s o -> p (b s o)")
        m_a, m_b, m_c, m_d = (scratch[:, k * NT * NU:(k + 1) * NT * NU].rearrange("p (i u) -> p i u", u=NU)
                                   for k in range(4))
        qbd = sb("qbd", [P, B, 2, P])
        mask = sb("mask", [P, B, SP_])
        w0g = sb("w0g", [P, NT, HD])
        w2g = sb("w2g", [P, NT, HD])
        w0bd = sb("w0bd", [P, NT, P])
        w2bd = sb("w2bd", [P, NT, P])
        x0T = sb("x0T", [P, 2, 2, P])
        sq = sb("sq", [P, 2, 12, HD])
        qk = sb("qk", [P, 2, 12, HD])
        tc_ = sb("tc_", [P, 2, 12, HD])
        ts_ = sb("ts_", [P, 2, 12, HD])
        qkv = sb("qkv", [P, 2, 512])
        st = sb("st", [P, 2, 8, 12])
        cosT = sb("cosT", [P, NT, 16])
        sinT = sb("sinT", [P, NT, 16])
        sc1 = sb("sc1", [P, 4, 16])
        CC = sb("CC", [P, NT, 4, 16])
        SS = sb("SS", [P, NT, 4, 16])
        m3 = sb("m3", [P, B])
        ia = sb("ia", [P, 2, NPOS], I32)
        fa = sb("fa", [P, 2, NPOS])
        i0 = sb("i0", [P, NT], I32)
        i2 = sb("i2", [P, NT], I32)
        it = sb("it", [P, NG], I32)
        fr = sb("fr", [P, 4, NG])
        tb = sb("tb", [P, NG], I32)
        tbf = sb("tbf", [P, NG])
        blkc = sb("blkc", [NU, P])
        blkw = sb("blkw", [P, NU])
        iov = sb("iov", [P, NG], I32)
        isc = sb("isc", [P, NT], I32)
        tk = sb("tk", [P, 12, NT])
        hi = sb("hi", [P, B])
        lo = sb("lo", [P, B])
        lo2 = sb("lo2", [P, B])
        mx = sb("mx", [P, B, 2])
        nmx = sb("nmx", [P, B, 2])
        ssum = sb("ssum", [P, B, 2])
        rs = sb("rs", [P, B, 2])
        late = win[:, :, :].rearrange("p g c -> p (g c)")
        late_at = [0]

        def late_sb(n, pattern, **dims):
            a = late_at[0]
            late_at[0] += n
            return late[:, a:a + n].rearrange(pattern, **dims)

        V = late_sb(4 * BPT * P, "p (a b c f) -> p a b c f", a=2, b=BPT, c=2)[0:HP]
        sm = late_sb(4 * SP_, "p (a b c) -> p a b c", a=2, b=2)
        pr = late_sb(4 * SP_, "p (a b c) -> p a b c", a=2, b=2)
        PT = late_sb(8 * P, "p (a b c d) -> p a b c d", a=2, b=2, c=2)[0:HP]
        oT = late_sb(4 * P, "p (a h f) -> p a h f", a=2, h=HPG)
        x1 = late_sb(2 * D, "p (a f) -> p a f", a=2)
        x2T = late_sb(4 * P, "p (a b f) -> p a b f", a=2, b=2)
        xaT = late_sb(2 * P, "p (a f) -> p a f", a=2)
        res = late_sb(2 * D, "p (a f) -> p a f", a=2)

        def C(name):
            a, w = C_AT[name]
            return cst[:, a:a + w]

        def I(name):
            a, w = I_AT[name]
            return ii[:, a:a + w]

        ident = C("ident")

        ps = [pb(f"ps{i}", [P, 512]) for i in range(8)]

        names = ("w3i x ints consts fdata wqkv wo w3 ball tab win0 win1 win2 w0 w2 pre "
                 "i0 it tbl blkc blkp msk idx i2 m3 rope trig sin w0bd w2bd qbz maskr "
                 "x0p x0s qkvp sqs ss rt rn qky t1 t2 rot vcp qtp qbe ktp kte vtp vtpe "
                 "scp smx nm ex rc pn ptp pte ob oe x1p x1e x2p x2e xap xae yp ye vch dch ach").split()
        S = {n: sem("s_" + n) for n in names}
        win_sem = [S["win0"], S["win1"], S["win2"]]
        w0_sem = [sem(f"s_w0_{i}") for i in range(NT)]
        w2_sem = [sem(f"s_w2_{i}") for i in range(NT)]
        sc_sem = [sem(f"s_sc_{i}") for i in range(2)]
        ov_sem = [sem(f"s_ov_{i}") for i in range(NG)]
        out_sem = [sem(f"s_out_{i}") for i in range(2)]

        block = ctx.enter_context(nc.Block())

        @block.sync
        def _(sp):
            sp.dma_start(ii[:, :], ints).then_inc(S["ints"], 16)
            sp.dma_start(cst[:, :], consts).then_inc(S["consts"], 16)
            sp.dma_start(xs[:, :, :], x_rows).then_inc(S["x"], 16)
            sp.wait_ge(win_sem[2], 16)
            sp.dma_start(kv_new, win[0:NU, 2, :]).then_inc(S["pre"], 16)
            for i in range(NT):
                sp.wait_ge(S["ye"], i + 1)
                sp.dma_start(out_rows[:, i, :], res[:, i % 2, :]).then_inc(out_sem[i % 2], 16)
            for j in range(2):
                sp.wait_ge(out_sem[j], 16 * NT // 2)

        @block.gpsimd
        def _(pool):
            def gather(dst, src, idx, s):
                pool.indirect_dma_start(out=dst, out_offset=None, in_=src,
                                        in_offset=bass.IndirectOffsetOnAxis(ap=idx, axis=0)).then_inc(s, 16)

            pool.wait_ge(S["it"], 1)
            for g in range(NG):
                n = GR[g]
                gather(tb[0:n, g:g + 1], table, it[0:n, g:g + 1], S["tab"])
            pool.wait_ge(S["i0"], 1)
            for i in range(2):
                gather(w0g[:, i, :], w0, i0[:, i:i + 1], w0_sem[i])
            pool.wait_ge(S["tab"], 16 * NG)
            for g in (2, 0, 1):
                n = GR[g]
                gather(win[0:n, g, :], kv, tb[0:n, g:g + 1], win_sem[g])
            for i in range(2, NT):
                gather(w0g[:, i, :], w0, i0[:, i:i + 1], w0_sem[i])
            nc.gpsimd.memset(qbd[:, :, :, :], 0.0).then_inc(S["qbz"], 1)
            pool.wait_ge(S["i2"], 1)
            for i in range(NT):
                gather(w2g[:, i, :], w2, i2[:, i:i + 1], w2_sem[i])
            pool.wait_ge(S["idx"], 1)
            pool.wait_ge(S["pre"], 16)
            for i in range(NT):
                for h0, nh in ((0, H), (H, G)):
                    pool.wait_ge(S["qky"], i + 1)
                    if i == 0:
                        pool.wait_ge(S["rope"], 1)
                    if i >= 2:
                        pool.wait_ge(S["rot"], 4 * (i - 1))
                    a = 0 if h0 == 0 else 2
                    nc.gpsimd.tensor_tensor(
                        ts_[:, i % 2, h0:h0 + nh, :], qk[:, i % 2, h0:h0 + nh, :],
                        SS[:, i, a:a + 2, :].rearrange("p a d -> p (a d)").unsqueeze(1).broadcast_to([P, nh, HD]),
                        ALU.mult).then_inc(S["t2"], 1)
                pool.wait_ge(S["rot"], 4 * (i + 1))
                pool.wait_ge(S["vcp"], i + 1)
                pool.indirect_dma_start(
                    out=kv_new.rearrange("u (o c) -> (u o) c", o=BLOCK),
                    out_offset=bass.IndirectOffsetOnAxis(ap=isc[:, i:i + 1], axis=0),
                    in_=qkv[:, i % 2, 256:512], in_offset=None,
                    bounds_check=NU * BLOCK - 1, oob_is_err=False).then_inc(sc_sem[i % 2], 16)
            for j in range(2):
                pool.wait_ge(sc_sem[j], 16 * NT // 2)
            for g in range(NG):
                n = GR[g]
                pool.indirect_dma_start(
                    out=win[0:n, g, :], out_offset=None, in_=kv_new,
                    in_offset=bass.IndirectOffsetOnAxis(ap=iov[0:n, g:g + 1], axis=0),
                    bounds_check=NU - 1, oob_is_err=False).then_inc(ov_sem[g], 16)
            for b in range(B):
                for p in range(2):
                    pool.wait_ge(S["rc"], b + 1)
                    nc.gpsimd.tensor_scalar(pr[:, b % 2, p, :], pr[:, b % 2, p, :], rs[:, b, p:p + 1], None,
                                            ALU.mult).then_inc(S["pn"], 1)

        def q_out(eng, i, gs):
            for g in gs:
                rows = slice(32 * g, 32 * g + 32)
                eng.wait_ge(S["qtp"], i + 1)
                if i == 0:
                    eng.wait_ge(S["qbz"], 1)
                dst = qbd[rows, BPT * i:BPT * i + BPT, g // 2, 64 * (g % 2):64 * (g % 2) + 64]\
                    .rearrange("p b (h t) -> p h b t", h=HPG)
                src = ps[4 + i % 2][rows, 0:256].rearrange("p (h b t) -> p h b t", h=HPG, b=BPT)
                if gs[0] == 0:
                    nc.scalar.activation(dst, src, ACT.Copy).then_inc(S["qbe"], 1)
                else:
                    nc.vector.tensor_copy(dst, src).then_inc(S["qbe"], 1)

        def kv_evac(eng, kind):
            n = 0
            for g in range(NG):
                ns = GR[g] // B
                for o4 in range(BLOCK // 4):
                    eng.wait_ge(S["vtp" if kind else "ktp"], n + 1)
                    src = ps[(4 if kind else 6) + n % 2][:, 0:4 * GR[g]].rearrange("p (o s b) -> p o s b", o=4, b=B)
                    for k in range(4):
                        dst = (VT if kind else KT)[:, :, 4 * g:4 * g + ns, 4 * o4 + k].rearrange("p b s -> p s b")
                        if kind:
                            x_ = nc.vector.tensor_copy(dst, src[:, k])
                        else:
                            x_ = nc.scalar.activation(dst, src[:, k], ACT.Copy)
                    x_.then_inc(S["vtpe" if kind else "kte"], 1)
                    n += 1

        def tail_act(act, i):
            act.wait_ge(S["x1p"], i + 1)
            if i >= 2:
                act.wait_ge(S["x2p"], i - 1)
            nc.scalar.activation(x1[:, i % 2, :], ps[5][:, 0:256], ACT.Copy).then_inc(S["x1e"], 1)
            act.wait_ge(S["yp"], i + 1)
            if i >= 2:
                act.wait_ge(out_sem[i % 2], 16 * (i // 2))
            nc.scalar.activation(res[:, i % 2, :], ps[6][:, 0:256], ACT.Copy).then_inc(S["ye"], 1)

        @block.scalar
        def _(act):
            act.dma_start(fd[:, :], fdata).then_inc(S["fdata"], 16)
            act.dma_start(wqkv_sb[:, :, :], wqkv).then_inc(S["wqkv"], 16)
            act.dma_start(wo_sb[:, :, :], wo).then_inc(S["wo"], 16)
            act.dma_start(w3_sb[:, :, :], w3).then_inc(S["w3"], 16)
            act.dma_start(ball_sb[:, :], ball).then_inc(S["ball"], 16)
            act.wait_ge(S["trig"], 1)
            nc.scalar.activation(sinT[:, :, :], sinT[:, :, :], ACT.Sin).then_inc(S["sin"], 1)
            nc.scalar.activation(cosT[:, :, :], cosT[:, :, :], ACT.Sin, bias=C("halfpi"), scale=-1.0)\
                .then_inc(S["sin"], 1)
            for i in range(NT):
                act.wait_ge(S["x0p"], i + 1)
                if i >= 2:
                    act.wait_ge(S["qkvp"], i - 1)
                nc.scalar.activation(x0T[:, i % 2, :, :].rearrange("p a b -> p (a b)"), ps[i % 2][:, 0:256],
                                     ACT.Copy).then_inc(S["x0s"], 1)
                act.wait_ge(S["qkvp"], i + 1)
                if i >= 2:
                    act.wait_ge(S["ss"], i - 1)
                nc.scalar.activation(sq[:, i % 2, :, :].rearrange("p a b -> p (a b)"), ps[2 + i % 2][:, 0:384],
                                     ACT.Square).then_inc(S["sqs"], 1)
                if i >= 2:
                    act.wait_ge(sc_sem[i % 2], 16 * (i // 2))
                nc.scalar.activation(qkv[:, i % 2, 384:512], ps[2 + i % 2][:, 384:512], ACT.Copy)\
                    .then_inc(S["vcp"], 1)
                act.wait_ge(S["ss"], i + 1)
                nc.scalar.activation(st[:, i % 2, 1, :], st[:, i % 2, 0, :], ACT.Sqrt).then_inc(S["rt"], 1)
                if i >= 1:
                    q_out(act, i - 1, (0, 1))
            q_out(act, NT - 1, (0, 1))
            kv_evac(act, 0)
            for n in range(B + 3):
                if n < B:
                    for p in range(2):
                        act.wait_ge(S["nm"], n + 1)
                        if n >= 2:
                            act.wait_ge(S["ptp"], n - 1)
                        nc.scalar.activation(pr[:, n % 2, p, :], sm[:, n % 2, p, :], ACT.Exp,
                                             bias=nmx[:, n, p:p + 1], scale=SCALE,
                                             accum_out=ssum[:, n, p:p + 1]).then_inc(S["ex"], 1)
                m = n - 1
                if 0 <= m < B:
                    act.wait_ge(S["ptp"], m + 1)
                    if m >= 2:
                        act.wait_ge(S["ob"], m - 1)
                    nc.scalar.activation(PT[:, m % 2, :, :, :].rearrange("p a b c -> p (a b c)"),
                                         ps[2 + m % 2][0:HP, :], ACT.Copy).then_inc(S["pte"], 1)
                m = n - 2
                if m >= 0 and m % BPT == BPT - 1:
                    tail_act(act, m // BPT)

        @block.vector
        def _(dve):
            chain = [0]

            def link(ins):
                chain[0] += 1
                ins.then_inc(S["dch"], 1)
                dve.wait_ge(S["dch"], chain[0])

            v = nc.vector
            dve.wait_ge(S["ints"], 16)
            dve.wait_ge(S["consts"], 16)
            v.tensor_scalar(ia[:, 0, :], ii[:, 0:NPOS], 4, None, ALU.arith_shift_right)
            link(v.tensor_scalar(ia[:, 1, :], ii[:, 0:NPOS], 15, None, ALU.bitwise_and))
            link(v.tensor_copy(fa[:, :, :], ia[:, :, :]))
            slot_row = fa[:, 0, NT:NT + 1]
            slot_b, off_b = fa[:, 0, NT + 1:NPOS], fa[:, 1, NT + 1:NPOS]
            off_tok = fa[:, 1, 0:NT]
            link(v.tensor_scalar(fr[:, 0, :], C("s8"), slot_row, 0.0, ALU.add, ALU.max))
            v.tensor_scalar(it[:, :], fr[:, 0, :], float(NBLK - 1), C("b257"), ALU.min, ALU.add)\
                .then_inc(S["it"], 1)
            v.tensor_scalar(i0[:, :], I("subj"), float(HD), C("t"), ALU.mult, ALU.add).then_inc(S["i0"], 1)
            v.tensor_scalar(i2[:, :], I("cond"), float(HD), C("t"), ALU.mult, ALU.add).then_inc(S["i2"], 1)
            ang, red = cosT, SS[:, :, 0, :]
            link(v.tensor_scalar(tk[:, 0, :], I("kvtok"), C("t"), None, ALU.add))
            link(v.tensor_tensor(ang[:, :, :], tk[:, 0, :].unsqueeze(2).broadcast_to([P, NT, 16]),
                                 C("invf").unsqueeze(1).broadcast_to([P, NT, 16]), ALU.mult))
            turns = CC[:, :, 0, :]
            link(v.tensor_scalar(turns, ang[:, :, :], 1.0 / 6.283185307179586, MAGIC, ALU.mult, ALU.add))
            link(v.tensor_scalar(turns, turns, MAGIC, None, ALU.subtract))
            src = ang[:, :, :]
            for part in TWO_PI:
                link(v.scalar_tensor_tensor(out=red, in0=turns, scalar=-part, in1=src,
                                            op0=ALU.mult, op1=ALU.add))
                src = red
            link(v.tensor_scalar(red, red, PI, -PI, ALU.min, ALU.max))
            v.tensor_copy(sinT[:, :, :], red)
            v.scalar_tensor_tensor(out=cosT[:, :, :], in0=red, scalar=-1.0, in1=red,
                                   op0=ALU.mult, op1=ALU.max).then_inc(S["trig"], 1)
            dve.wait_ge(S["fdata"], 16)
            link(v.tensor_scalar(sc1[:, :, :].rearrange("p a b -> p (a b)"), fd[:, 0:64], 1.0, None, ALU.add))
            dve.wait_ge(S["sin"], 2)
            for dst, src in ((CC, cosT), (SS, sinT)):
                ins = v.tensor_tensor(dst[:, :, :, :], src[:, :, :].unsqueeze(2).broadcast_to([P, NT, 4, 16]),
                                      sc1[:, :, :].unsqueeze(1).broadcast_to([P, NT, 4, 16]), ALU.mult)
            ins.then_inc(S["rope"], 1)
            v.tensor_scalar(m3[:, :], I("adapt"), C("aid"), fd[:, 64:65], ALU.is_equal, ALU.mult)
            dve.wait_ge(S["tab"], 16 * NG)
            v.tensor_copy(blkc[:, :], tb[0:NU, 2:3].broadcast_to([NU, P])).then_inc(S["blkc"], 1)
            v.tensor_copy(tbf[:, 0:2], tb[:, 0:2])
            link(v.tensor_copy(tbf[0:NU, 2:3], tb[0:NU, 2:3]))
            link(v.tensor_scalar(tk[:, 1, :], off_tok, C("t"), None, ALU.add))
            link(v.tensor_scalar(tk[:, 2, :], tk[:, 1, :], 15.5, None, ALU.is_gt))
            link(v.scalar_tensor_tensor(out=tk[:, 3, :], in0=tk[:, 1, :], scalar=31.5, in1=tk[:, 2, :],
                                        op0=ALU.is_gt, op1=ALU.add))
            link(v.scalar_tensor_tensor(out=tk[:, 4, :], in0=tk[:, 3, :], scalar=-16.0, in1=tk[:, 1, :],
                                        op0=ALU.mult, op1=ALU.add))
            link(v.scalar_tensor_tensor(out=tk[:, 5, :], in0=tk[:, 3, :], scalar=float(B), in1=C("btok"),
                                        op0=ALU.mult, op1=ALU.add))
            link(v.tensor_tensor(m_c[:, 0, :].rearrange("p (k b) -> p k b", k=NW),
                                 C("k16").rearrange("p (k b) -> p k b", k=NW),
                                 off_b.unsqueeze(1).broadcast_to([P, NW, B]), ALU.subtract))
            dve.wait_ge(S["blkp"], 1)
            link(v.tensor_copy(blkw[:, :], ps[7][:, 0:NU]))

            def row(a, n=NT):
                return a.unsqueeze(1).broadcast_to([P, n, NU])

            def col(a, n=NT):
                return a.unsqueeze(2).broadcast_to([P, n, NU])

            link(v.memset(m_a[:, 0:NG, :], 0.0))
            link(v.tensor_tensor(m_a[:, 0:2, :], row(blkw[:, :], 2), col(tbf[:, 0:2], 2), ALU.is_equal))
            link(v.tensor_tensor(m_a[0:NU, 2, :], blkw[0:NU, :], tbf[0:NU, 2:3].broadcast_to([NU, NU]),
                                 ALU.is_equal))
            link(v.tensor_tensor(m_a[:, 0:NG, :], m_a[:, 0:NG, :], row(C("u1"), NG), ALU.mult))
            link(v.tensor_reduce(fr[:, 1, :], m_a[:, 0:NG, :], AX_X, ALU.max))
            link(v.tensor_scalar(fr[:, 2, :], fr[:, 1, :], 0.5, 4096.0, ALU.is_lt, ALU.mult))
            link(v.scalar_tensor_tensor(out=iov[:, :], in0=fr[:, 1, :], scalar=-1.0, in1=fr[:, 2, :],
                                        op0=ALU.add, op1=ALU.add))
            link(v.tensor_tensor(m_a[:, :, :], row(C("u1")), col(tk[:, 5, :]), ALU.subtract))
            link(v.tensor_scalar(m_a[:, :, :], m_a[:, :, :], 1.0, None, ALU.is_equal))
            link(v.tensor_tensor(m_a[:, :, :], m_a[:, :, :], row(blkw[:, :]), ALU.mult))
            link(v.tensor_reduce(tk[:, 6, :], m_a[:, :, :], AX_X, ALU.add))
            link(v.tensor_tensor(m_a[:, :, :], row(blkw[:, :]), col(tk[:, 6, :]), ALU.is_equal))
            link(v.tensor_tensor(m_b[:, :, :], m_a[:, :, :], row(C("u1")), ALU.mult))
            link(v.tensor_reduce(tk[:, 7, :], m_b[:, :, :], AX_X, ALU.max))
            link(v.tensor_tensor(m_b[:, :, :], row(m_c[:, 0, :]), col(tk[:, 4, :]), ALU.add))
            link(v.tensor_scalar(m_d[:, :, :], m_b[:, :, :], -15.5, None, ALU.add))
            link(v.scalar_tensor_tensor(out=m_c[:, :, :], in0=m_d[:, :, :], scalar=-1.0, in1=m_d[:, :, :],
                                        op0=ALU.mult, op1=ALU.max))
            link(v.scalar_tensor_tensor(out=m_a[:, :, :], in0=m_c[:, :, :], scalar=16.0, in1=m_a[:, :, :],
                                        op0=ALU.is_lt, op1=ALU.mult))
            link(v.scalar_tensor_tensor(out=m_b[:, :, :], in0=m_b[:, :, :], scalar=1.0, in1=row(C("b32")),
                                        op0=ALU.add, op1=ALU.add))
            link(v.tensor_tensor(m_b[:, :, :], m_b[:, :, :], m_a[:, :, :], ALU.mult))
            link(v.tensor_reduce(tk[:, 8, :], m_b[:, :, :], AX_X, ALU.max))
            link(v.tensor_tensor(tk[:, 9, :], tk[:, 8, :], C("j1"), ALU.is_gt))
            link(v.scalar_tensor_tensor(out=tk[:, 10, :], in0=tk[:, 7, :], scalar=float(BLOCK), in1=tk[:, 4, :],
                                        op0=ALU.mult, op1=ALU.add))
            link(v.scalar_tensor_tensor(out=tk[:, 10, :], in0=tk[:, 9, :], scalar=65536.0, in1=tk[:, 10, :],
                                        op0=ALU.mult, op1=ALU.add))
            v.tensor_scalar(isc[:, :], tk[:, 10, :], -float(BLOCK), None, ALU.add).then_inc(S["idx"], 1)

            v.tensor_scalar(hi[:, :], off_b, C("t128"), None, ALU.add)
            link(v.tensor_scalar(lo[:, :], slot_b, -float(BLOCK), float(WINDOW - 1), ALU.mult, ALU.add))
            link(v.scalar_tensor_tensor(out=lo2[:, :], in0=off_b, scalar=C("t"), in1=lo[:, :],
                                        op0=ALU.add, op1=ALU.max))

            def phase_a(i):
                par = i % 2
                dve.wait_ge(w0_sem[i], 16)
                link(v.tensor_tensor(w0bd[:, i, :].rearrange("p (b d) -> p b d", b=BPT),
                                     w0g[:, i, :].unsqueeze(1).broadcast_to([P, BPT, HD]),
                                     C("bdmask").rearrange("p (b d) -> p b d", b=BPT), ALU.mult))
                v.tensor_tensor(w0bd[:, i, :], w0bd[:, i, :], ident, ALU.add).then_inc(S["w0bd"], 1)

            phase_a(0)
            for i in range(NT):
                par = i % 2
                if i + 1 < NT:
                    phase_a(i + 1)
                for b in range(BPT * i, BPT * i + BPT):
                    link(v.tensor_scalar(mask[:, b, :], C("rel"), hi[:, b:b + 1], None, ALU.is_gt))
                    link(v.scalar_tensor_tensor(out=mask[:, b, :], in0=C("rel"), scalar=lo2[:, b:b + 1],
                                                in1=mask[:, b, :], op0=ALU.is_le, op1=ALU.add))
                    v.tensor_scalar(mask[:, b, :], mask[:, b, :], -BIG, None, ALU.mult).then_inc(S["msk"], 1)
                dve.wait_ge(S["sqs"], i + 1)
                link(v.tensor_reduce(st[:, par, 2, :], sq[:, par, :, :], AX_X, ALU.add))
                v.tensor_scalar(st[:, par, 0, :], st[:, par, 2, :], 1.0 / HD, EPS, ALU.mult, ALU.add)\
                    .then_inc(S["ss"], 1)
                dve.wait_ge(S["rt"], i + 1)
                link(v.reciprocal(st[:, par, 3, :], st[:, par, 1, :]))
                link(v.tensor_tensor(st[:, par, 4, :], st[:, par, 3, :], st[:, par, 3, :], ALU.mult))
                link(v.tensor_tensor(st[:, par, 5, :], st[:, par, 4, :], st[:, par, 0, :], ALU.mult))
                link(v.tensor_scalar(st[:, par, 6, :], st[:, par, 5, :], -0.5, 1.5, ALU.mult, ALU.add))
                link(v.tensor_tensor(st[:, par, 7, :], st[:, par, 3, :], st[:, par, 6, :], ALU.mult))
                if i >= 2:
                    dve.wait_ge(S["t2"], 2 * (i - 1))
                v.tensor_tensor(qk[:, par, :, :], ps[2 + par][:, 0:384].rearrange("p (h d) -> p h d", d=HD),
                                st[:, par, 7, :].unsqueeze(2).broadcast_to([P, 12, HD]), ALU.mult)\
                    .then_inc(S["qky"], 1)
                dve.wait_ge(S["qky"], i + 1)
                for h0, nh, a in ((0, H, 0), (H, G, 2)):
                    ins = v.tensor_tensor(
                        tc_[:, par, h0:h0 + nh, :], qk[:, par, h0:h0 + nh, :],
                        CC[:, i, a:a + 2, :].rearrange("p a d -> p (a d)").unsqueeze(1).broadcast_to([P, nh, HD]),
                        ALU.mult)
                link(ins)
                dve.wait_ge(S["t2"], 2 * (i + 1))
                if i >= 2:
                    dve.wait_ge(S["qtp"], i - 1)
                    dve.wait_ge(sc_sem[i % 2], 16 * (i // 2))
                r = qkv[:, par, 0:384].rearrange("p (h d) -> p h d", d=HD)
                v.tensor_tensor(r[:, :, 0:16], tc_[:, par, :, 0:16], ts_[:, par, :, 16:32], ALU.subtract)\
                    .then_inc(S["rot"], 2)
                v.tensor_tensor(r[:, :, 16:32], tc_[:, par, :, 16:32], ts_[:, par, :, 0:16], ALU.add)\
                    .then_inc(S["rot"], 2)
                if i >= 1:
                    q_out(dve, i - 1, (2, 3))
            q_out(dve, NT - 1, (2, 3))
            dve.wait_ge(S["w3"], 16)
            for c in range(2):
                v.tensor_tensor(w3_sb[:, c, c * P:(c + 1) * P], w3_sb[:, c, c * P:(c + 1) * P], ident, ALU.add)\
                    .then_inc(S["w3i"], 1)
            for i in range(NT):
                dve.wait_ge(w2_sem[i], 16)
                link(v.tensor_tensor(w2bd[:, i, :].rearrange("p (b d) -> p b d", b=BPT),
                                     w2g[:, i, :].unsqueeze(1).broadcast_to([P, BPT, HD]),
                                     C("bdmask").rearrange("p (b d) -> p b d", b=BPT), ALU.mult))
                v.tensor_tensor(w2bd[:, i, :], w2bd[:, i, :], ident, ALU.add).then_inc(S["w2bd"], 1)
            kv_evac(dve, 1)

            for n in range(B + 3):
                if n < B:
                    for p in range(2):
                        dve.wait_ge(S["scp"], n + 1)
                        dve.wait_ge(S["msk"], n + 1)
                        if n >= 2:
                            dve.wait_ge(S["ex"], 2 * (n - 1))
                        ins = v.tensor_tensor_reduce(
                            out=sm[:, n % 2, p, :], in0=ps[n % 2][:, p * SP_:(p + 1) * SP_], in1=mask[:, n, :],
                            scale=1.0, scalar=-3e38, op0=ALU.add, op1=ALU.max, accum_out=mx[:, n, p:p + 1])
                        ins.then_inc(S["smx"], 1)
                    dve.wait_ge(S["smx"], 2 * (n + 1))
                    v.tensor_scalar(nmx[:, n, :], mx[:, n, :], -SCALE, None, ALU.mult).then_inc(S["nm"], 1)
                    if n % 2 == 0:
                        dve.wait_ge(S["vtp"], 12 + n // 2 + 1)
                        if n >= 2 * BPT:
                            dve.wait_ge(S["ob"], n - 2 * BPT + 2)
                        v.tensor_copy(V[:, (n // BPT) % 2, n % BPT:n % BPT + 2, :, :].rearrange("p a b c -> p (a b c)"),
                                      ps[4][0:HP, :]).then_inc(S["vtpe"], 1)
                m = n - 1
                if 0 <= m < B:
                    dve.wait_ge(S["ex"], 2 * (m + 1))
                    v.reciprocal(rs[:, m, :], ssum[:, m, :]).then_inc(S["rc"], 1)
                m = n - 2
                if m >= 0 and m % BPT == BPT - 1:
                    i = m // BPT
                    par = i % 2
                    dve.wait_ge(S["ob"], m + 1)
                    if i >= 2:
                        dve.wait_ge(S["x1p"], i - 1)
                    v.tensor_copy(oT[:, par, :, :].rearrange("p h (b t) -> p b h t", b=BPT),
                                  ps[7][:, 0:256].rearrange("p (b h t) -> p b h t", b=BPT, h=HPG))\
                        .then_inc(S["oe"], 1)
                    dve.wait_ge(S["x2p"], i + 1)
                    if i >= 2:
                        dve.wait_ge(S["yp"], i - 1)
                    v.tensor_copy(x2T[:, par, :, :].rearrange("p a b -> p (a b)"), ps[5][:, 256:512])\
                        .then_inc(S["x2e"], 1)
                    dve.wait_ge(S["xap"], i + 1)
                    v.tensor_tensor(xaT[:, par, :].rearrange("p (b t) -> p b t", b=BPT),
                                    ps[5][:, 0:P].rearrange("p (b t) -> p b t", b=BPT),
                                    m3[:, BPT * i:BPT * i + BPT].unsqueeze(2).broadcast_to([P, BPT, T]),
                                    ALU.mult).then_inc(S["xae"], 1)

        @block.tensor
        def _(pe):
            mm = nc.tensor.matmul
            pe.wait_ge(S["consts"], 16)
            pe.wait_ge(S["blkc"], 1)
            mm(ps[7][:, 0:NU], blkc[:, :], ident[0:NU, 0:NU], start=True, stop=True).then_inc(S["blkp"], 1)
            pe.wait_ge(S["x"], 16)

            def x0(i):
                pe.wait_ge(S["w0bd"], i + 1)
                if i >= 2:
                    pe.wait_ge(S["x0s"], i - 1)
                for c in range(2):
                    last = mm(ps[i % 2][:, c * P:(c + 1) * P], xs[:, i, c * P:(c + 1) * P], w0bd[:, i, :],
                              start=True, stop=True)
                last.then_inc(S["x0p"], 1)

            def q_transpose(i):
                pe.wait_ge(S["rot"], 4 * (i + 1))
                if i >= 2:
                    pe.wait_ge(S["qbe"], 4 * (i - 1))
                for h in range(HPG):
                    last = nc.tensor.transpose(ps[4 + i % 2][:, h * P:(h + 1) * P], qkv[:, i % 2, h * P:(h + 1) * P],
                                               ident)
                last.then_inc(S["qtp"], 1)

            x0(0)
            for i in range(NT):
                if i + 1 < NT:
                    x0(i + 1)
                pe.wait_ge(S["x0s"], i + 1)
                if i == 0:
                    pe.wait_ge(S["wqkv"], 16)
                if i >= 2:
                    pe.wait_ge(S["qky"], i - 1)
                    pe.wait_ge(S["vcp"], i - 1)
                for c in range(2):
                    last = mm(ps[2 + i % 2][:, :], x0T[:, i % 2, c, :], wqkv_sb[:, c, :], start=(c == 0),
                              stop=(c == 1))
                last.then_inc(S["qkvp"], 1)
                if i >= 1:
                    q_transpose(i - 1)
            q_transpose(NT - 1)

            n = 0
            pe.wait_ge(S["qbe"], 4 * NT)
            for g in range(NG):
                m = GR[g]
                pe.wait_ge(ov_sem[g], 16)
                for o4 in range(BLOCK // 4):
                    for kind in range(2):
                        if n >= 2:
                            pe.wait_ge(S["vtpe" if kind else "kte"], n - 1)
                        for k in range(4):
                            a = (4 * o4 + k) * KVW + kind * P
                            last = nc.tensor.transpose(ps[(4 if kind else 6) + n % 2][:, k * m:(k + 1) * m],
                                                       win[0:m, g, a:a + P], ident[0:m, 0:m])
                        last.then_inc(S["vtp" if kind else "ktp"], 1)
                    n += 1
            pe.wait_ge(S["kte"], 12)
            pe.wait_ge(S["vtpe"], 12)

            def scores(b):
                if b >= 2:
                    pe.wait_ge(S["smx"], 2 * (b - 1))
                for p in range(2):
                    last = mm(ps[b % 2][:, p * SP_:(p + 1) * SP_], qbd[:, b, p, :],
                              KT[:, b, :, :].rearrange("p s o -> p (s o)"), start=True, stop=True)
                last.then_inc(S["scp"], 1)
                if b % 2 == 0:
                    if b >= 2:
                        pe.wait_ge(S["vtpe"], 12 + b // 2)
                    for k in range(4):
                        bb, c = b + k // 2, k % 2
                        last = nc.tensor.transpose(
                            ps[4][0:HP, k * P:(k + 1) * P],
                            VT[:, bb, :, :].rearrange("p s o -> p (s o)")[:, c * HP:(c + 1) * HP], ident)
                    last.then_inc(S["vtp"], 1)

            def p_transpose(b):
                pe.wait_ge(S["pn"], 2 * (b + 1))
                if b >= 2:
                    pe.wait_ge(S["pte"], b - 1)
                for c in range(2):
                    for p in range(2):
                        last = nc.tensor.transpose(ps[2 + b % 2][0:HP, (2 * c + p) * P:(2 * c + p + 1) * P],
                                                   pr[:, b % 2, p, c * HP:(c + 1) * HP], ident)
                last.then_inc(S["ptp"], 1)

            def pv(b):
                pe.wait_ge(S["pte"], b + 1)
                pe.wait_ge(S["vtpe"], 12 + b // 2 + 1)
                j = b % BPT
                if j == 0 and b >= BPT:
                    pe.wait_ge(S["oe"], b // BPT)
                for g in range(G):
                    for c in range(2):
                        last = mm(ps[7][32 * g:32 * g + 32, 64 * j:64 * j + 64],
                                  V[:, (b // BPT) % 2, j, c, 32 * g:32 * g + 32],
                                  PT[:, b % 2, c, g // 2, 64 * (g % 2):64 * (g % 2) + 64],
                                  start=(c == 0), stop=(c == 1))
                last.then_inc(S["ob"], 1)

            def tail(i):
                par = i % 2
                if i == 0:
                    for s in ("wo", "ball"):
                        pe.wait_ge(S[s], 16)
                    pe.wait_ge(S["w3i"], 2)
                pe.wait_ge(S["oe"], i + 1)
                if i >= 1:
                    pe.wait_ge(S["xae"], i)
                mm(ps[5][:, 0:256], w0bd[:, i, :], xs[:, i, :], start=True, stop=False)
                for h in range(HPG):
                    last = mm(ps[5][:, 0:256], oT[:, par, h, :], wo_sb[:, h, :], start=False, stop=(h == HPG - 1))
                last.then_inc(S["x1p"], 1)
                pe.wait_ge(S["x1e"], i + 1)
                pe.wait_ge(S["w2bd"], i + 1)
                for c in range(2):
                    last = mm(ps[5][:, 256 + c * P:256 + (c + 1) * P], x1[:, par, c * P:(c + 1) * P], w2bd[:, i, :],
                              start=True, stop=True)
                last.then_inc(S["x2p"], 1)
                pe.wait_ge(S["x2e"], i + 1)
                for c in range(2):
                    last = mm(ps[5][:, 0:P], w3_sb[:, c, 256:384], x2T[:, par, c, :], start=(c == 0),
                              stop=(c == 1))
                last.then_inc(S["xap"], 1)
                if i >= 1:
                    pe.wait_ge(S["ye"], i)
                for c in range(2):
                    mm(ps[6][:, 0:256], x2T[:, par, c, :], w3_sb[:, c, 0:256], start=(c == 0), stop=False)
                pe.wait_ge(S["xae"], i + 1)
                mm(ps[6][:, 0:256], xaT[:, par, :], ball_sb[:, :], start=False, stop=True).then_inc(S["yp"], 1)

            for n in range(B + 3):
                if n < B:
                    scores(n)
                if 0 <= n - 1 < B:
                    p_transpose(n - 1)
                if 0 <= n - 2 < B:
                    pv(n - 2)
                    if (n - 2) % BPT == BPT - 1:
                        tail((n - 2) // BPT)


def _constants(np):
    p = np.arange(P)
    c = np.zeros((P, NC_), np.float32)

    def put(name, a):
        o, w = C_AT[name]
        c[:, o:o + w] = a

    put("ident", np.eye(P))
    put("bdmask", p[:, None] // HD == p[None, :] // HD)
    u = np.arange(NU)
    put("u1", u + 1)
    put("k16", BLOCK * (u // B))
    put("b32", T * (u % B))
    put("rel", np.arange(SP_))
    half = HD // 2
    put("invf", np.float32(1.0) / np.float32(10000.0) ** (np.arange(half, dtype=np.float32) / np.float32(half)))
    put("s8", BPT * np.arange(NG)[None, :] + (p // B)[:, None] - WINDOW // BLOCK)
    put("b257", (p % B * NBLK)[:, None])
    put("t", (p % T)[:, None])
    put("t128", (p % T + WINDOW)[:, None])
    put("j1", P * np.arange(NT)[None, :] + p[:, None] + 1)
    put("btok", BPT * np.arange(NT)[None, :] + (p // T)[:, None])
    put("aid", (p // 16)[:, None])
    put("halfpi", np.pi / 2)
    put("eps", EPS)
    return c


def kernel(**inputs):
    import numpy as np
    import concourse.bacc as bacc
    from concourse.bass_utils import run_bass_kernel_spmd as run

    a = {k: np.asarray(v) for k, v in inputs.items()}

    def tok(v):
        return np.repeat(v.reshape(NT, BPT).T, T, axis=0)

    def row(v):
        return np.broadcast_to(v[None, :], (P, B))

    kvl = a["itok_B_37_3939"].astype(np.int32)
    ints = np.concatenate([tok(kvl), np.tile(kvl, BPT)[:, None], row(kvl), tok(a["itok_B_0_7"].astype(np.int32)),
                           tok(a["itok_B_1_198"].astype(np.int32)), row(a["itok_B_0_6"].astype(np.int32))], axis=1)
    kvc = np.empty((NPHYS, BLOCK, 2, G, HD), np.float32)
    kvc[:, :, 0] = a["L1_cond_k_blocks"].transpose(0, 2, 1, 3)
    kvc[:, :, 1] = a["L1_cond_v_blocks"].transpose(0, 2, 1, 3)
    fdata = np.concatenate([np.broadcast_to(a["L1_cond_q_norm_scale"][None, :], (P, HD)),
                            np.broadcast_to(a["L1_cond_k_norm_scale"][None, :], (P, HD)),
                            np.repeat(a["L3_cond_scalings"], 16)[:, None]], axis=1)

    def split(w):
        return w.reshape(2, P, -1).transpose(1, 0, 2)

    wq = a["L1_cond_Wq"].reshape(G, HPG, HD, D).transpose(1, 0, 2, 3).reshape(H * HD, D)
    wqkv = split(np.concatenate([wq, a["L1_cond_Wk"], a["L1_cond_Wv"]], axis=0).T)
    wo = a["L1_cond_Wo"].T.reshape(G, HPG, HD, D).transpose(0, 2, 1, 3).reshape(P, HPG, D)
    w3 = split(np.concatenate([a["L3_cond_W"].T, a["L3_cond_A"].reshape(P, D).T], axis=1))
    arrays = {
        "x": a["x"].reshape(B * T, D), "ints": ints, "consts": _constants(np), "fdata": fdata,
        "table": a["itok_Bx257_0_4111"].astype(np.int32).reshape(B * NBLK, 1),
        "kv": kvc.reshape(NPHYS, BLOCK * KVW),
        "w0": a["L0_cond_weights"].reshape(-1, HD), "w2": a["L2_cond_weights"].reshape(-1, HD),
        "wqkv": wqkv, "wo": wo, "w3": w3,
        "ball": a["L3_cond_Bm"].transpose(0, 2, 1).reshape(P, D),
    }
    arrays = {k: np.ascontiguousarray(v) for k, v in arrays.items()}
    nc = bacc.Bacc("TRN2", target_bir_lowering=False, num_devices=1)
    aps = {k: nc.dram_tensor(k, v.shape, mybir.dt.from_np(v.dtype), kind="ExternalInput").ap()
           for k, v in arrays.items()}
    out = nc.dram_tensor("out", (B * T, D), F32, kind="ExternalOutput").ap()
    program(nc, aps["x"], aps["ints"], aps["consts"], aps["fdata"], aps["table"], aps["kv"], aps["w0"], aps["w2"],
            aps["wqkv"], aps["wo"], aps["w3"], aps["ball"], out)
    r = run(nc, [arrays], core_ids=[0])
    return np.asarray(r.results[0]["out"]).reshape(B, T, D)
```

```python
import concourse.bass as bass
from concourse import mybir
from contextlib import ExitStack

F32 = mybir.dt.float32
I32 = mybir.dt.int32
U32 = mybir.dt.uint32
ALU = mybir.AluOpType
ACT = mybir.ActivationFunctionType
AX_X = mybir.AxisListType.X

P = 128
B, T, D = 32, 32, 256
G, HPG, HD = 4, 2, 32
H = G * HPG
BLOCK, NBLK, NPHYS = 16, 257, 4112
WINDOW = 128
SCALE = 256.0 ** -0.5
EPS = 1e-6
NT = B * T // P
BPT = P // T
NS = WINDOW // BLOCK + 3
NW = 3
SP_ = NS * BLOCK
HP = SP_ // 2
NU = NW * B
NG = 3
GR = [128, 128, NU]
KVW = 2 * G * HD
BIG = 1e30
PI = 3.1415925
TWO_PI = (6.28125, 0.0019350051879882812, 3.019916050561733e-07)
MAGIC = 12582912.0

_C = [("ident", 128), ("u1", NU), ("j0", NU), ("invf", 16), ("s8", NG), ("b257", 1), ("t", 1), ("j1", NT),
      ("aid", 1), ("halfpi", 1), ("eps", 1)]
C_AT, NC_ = {}, 0
for _n, _w in _C:
    C_AT[_n] = (NC_, _w)
    NC_ += _w
_I = [("kvtok", NT), ("kvrow", 1), ("kvb", B), ("subj", B), ("cond", B), ("adapt", B)]
I_AT, NI_ = {}, 0
for _n, _w in _I:
    I_AT[_n] = (NI_, _w)
    NI_ += _w
NPOS = NT + 1 + B
NMASK = WINDOW // BLOCK + 1
NA = BLOCK - 1 + T
HT = NT // 2
MR = 8
PR = 3


def program(nc, x, ints, consts, fdata, table, masks, kv, w0, w2, wqkv, wo, w3, ball, out):
    kv_new = nc.dram_tensor("kv_new", (NU, BLOCK * KVW), F32, kind="Internal").ap()
    x_rows = x.rearrange("(i p) f -> p i f", p=P)
    out_rows = out.rearrange("(i p) f -> p i f", p=P)

    ctx = ExitStack()
    with ctx:
        def sb(name, shape, dt=F32):
            return ctx.enter_context(nc.sbuf_tensor(name, shape, dt))

        def pb(name, shape, dt=F32):
            return ctx.enter_context(nc.psum_tensor(name, shape, dt))

        def sem(name):
            return ctx.enter_context(nc.semaphore(name))

        cst = sb("cst", [P, NC_])
        ii = sb("ii", [P, NI_], I32)
        fd = sb("fd", [P, 65])
        xs = sb("xs", [P, NT, D])
        wqkv_sb = sb("wqkv_sb", [P, 2, 512])
        wo_sb = sb("wo_sb", [P, HPG, D])
        w3_sb = sb("w3_sb", [P, 2, 384])
        ball_sb = sb("ball_sb", [P, D])
        win = sb("win", [P, NG, BLOCK * KVW])
        KT = sb("KT", [P, B, NS, BLOCK])
        VT = sb("VT", [P, B, NS, BLOCK])
        qT = sb("qT", [P, B, HPG, T])
        mask = sb("mask", [P, MR, SP_])
        w0bd = sb("w0bd", [P, NT, P])
        w2bd = sb("w2bd", [P, NT, P])
        x0T = sb("x0T", [P, 2, 2, P])
        qk = sb("qk", [P, NT, (H + G) * HD])
        kvn = sb("kvn", [P, NT, KVW])
        sq = sb("sq", [P, HT, H * HD])
        yn = sb("yn", [P, HT, H * HD])
        ts_ = sb("ts_", [P, HT, H * HD])
        st = sb("st", [P, 8, HT * H])
        cosT = sb("cosT", [P, NT, 16])
        sinT = sb("sinT", [P, NT, 16])
        sc1 = sb("sc1", [P, 4, 16])
        CC = sb("CC", [P, NT, 4, 16])
        SS = sb("SS", [P, NT, 4, 16])
        m3 = sb("m3", [P, B])
        ia = sb("ia", [P, 2, NPOS], I32)
        fa = sb("fa", [P, 2, NPOS])
        it = sb("it", [P, NG], I32)
        fr = sb("fr", [P, 4, NG])
        tb = sb("tb", [P, NG], I32)
        tbf = sb("tbf", [P, NG])
        rep = sb("rep", [NU, 2, P])
        wr = sb("wr", [P, 2, NU])
        wt = sb("wt", [P, 2, NW, NT])
        iov = sb("iov", [P, NG], I32)
        isc = sb("isc", [P, NT], I32)
        im = sb("im", [P, B], I32)
        imf = sb("imf", [P, B])
        tk = sb("tk", [P, 8, NT])
        tw = sb("tw", [P, 2, 2, NT])
        tj = sb("tj", [P, NU])
        mx = sb("mx", [P, B, 2])
        nmx = sb("nmx", [P, B, 2])
        ssum = sb("ssum", [P, B, 2])
        rs = sb("rs", [P, B, 2])
        scratch = VT[:, :, :, :].rearrange("p b s o -> p (b s o)")
        m_a, m_b, m_c = (scratch[:, k * NT * NU:(k + 1) * NT * NU].rearrange("p (i u) -> p i u", u=NU)
                         for k in range(3))
        late = win[:, :, :].rearrange("p g c -> p (g c)")
        late_at = [0]

        def late_sb(n, pattern, **dims):
            a = late_at[0]
            late_at[0] += n
            return late[:, a:a + n].rearrange(pattern, **dims)

        V = late_sb(4 * BPT * P, "p (a b c f) -> p a b c f", a=2, b=BPT, c=2)[0:HP]
        sm = late_sb(4 * SP_, "p (a b c) -> p a b c", a=2, b=2)
        pr = late_sb(2 * PR * SP_, "p (a b c) -> p a b c", a=PR, b=2)
        PT = late_sb(8 * P, "p (a b c d) -> p a b c d", a=2, b=2, c=2)[0:HP]
        oT = late_sb(4 * P, "p (a h f) -> p a h f", a=2, h=HPG)
        x1 = late_sb(2 * D, "p (a f) -> p a f", a=2)
        x2T = late_sb(4 * P, "p (a b f) -> p a b f", a=2, b=2)
        xaT = late_sb(2 * P, "p (a f) -> p a f", a=2)
        res = late_sb(2 * D, "p (a f) -> p a f", a=2)

        def C(name):
            a, w = C_AT[name]
            return cst[:, a:a + w]

        def I(name):
            a, w = I_AT[name]
            return ii[:, a:a + w]

        ident = C("ident")

        ps = [pb(f"ps{i}", [P, 512]) for i in range(8)]
        PS_S, PS_P, PS_V, PS_O, PS_X, PS_Y = (0, 1), (2, 3), 4, 5, 6, 7

        names = ("ints consts x fdata wqkv wo w3 ball tab win0 win1 win2 pre it rep repp im trig sin rope idx "
                 "w0z w2z w0bd w2bd w3i x0p x0s qkvp qke kve sqs ss rt rot qtp qte ktp kte vtp vte "
                 "scp smx nm ex rc pn ptp pte ob oe x1p x1e x2p x2e xap xae yp ye dch").split()
        S = {n: sem("s_" + n) for n in names}
        win_sem = [S["win0"], S["win1"], S["win2"]]
        w0_sem = [sem(f"s_w0_{i}") for i in range(NT)]
        w2_sem = [sem(f"s_w2_{i}") for i in range(NT)]
        ov_sem = [sem(f"s_ov_{i}") for i in range(NG)]
        mask_sem = [sem(f"s_mask_{i}") for i in range(MR)]
        sc_sem = sem("s_sc")
        out_sem = [sem(f"s_out_{i}") for i in range(2)]

        block = ctx.enter_context(nc.Block())

        LAG_P, LAG_O = 2, 3

        def tail_tile(n, stage):
            m = n - LAG_O - stage
            return m // BPT if m >= 0 and m % BPT == BPT - 1 and m < B else None

        STEPS = B + LAG_O + 6

        @block.sync
        def _(sp):
            sp.dma_start(ii[:, :], ints).then_inc(S["ints"], 16)
            sp.dma_start(cst[:, :], consts).then_inc(S["consts"], 16)
            sp.dma_start(xs[:, :, :], x_rows).then_inc(S["x"], 16)

            def mixing(dst, w, col, n, sems):
                a, _w = I_AT[col]
                for b in range(B):
                    r = sp.value_load(ii[0:1, a + b:a + b + 1], min_val=0, max_val=n - 1)
                    j = b % BPT
                    sp.dma_start(dst[32 * j:32 * j + 32, b // BPT, 32 * j:32 * j + 32], w[bass.ds(r, 1), :, :]
                                 .rearrange("a c d -> (a c) d")).then_inc(sems[b // BPT], 16)

            sp.wait_ge(S["ints"], 16)
            sp.wait_ge(S["w0z"], 1)
            mixing(w0bd, w0, "subj", 8, w0_sem)
            sp.wait_ge(win_sem[2], 16)
            sp.dma_start(kv_new, win[0:NU, 2, :]).then_inc(S["pre"], 16)
            sp.wait_ge(S["w2z"], 1)
            mixing(w2bd, w2, "cond", 200, w2_sem)
            for i in range(NT):
                sp.wait_ge(S["ye"], i + 1)
                sp.dma_start(out_rows[:, i, :], res[:, i % 2, :]).then_inc(out_sem[i % 2], 16)
            for j in range(2):
                sp.wait_ge(out_sem[j], 16 * NT // 2)

        @block.gpsimd
        def _(pool):
            def gather(dst, src, idx, s, **kw):
                pool.indirect_dma_start(out=dst, out_offset=None, in_=src,
                                        in_offset=bass.IndirectOffsetOnAxis(ap=idx, axis=0), **kw).then_inc(s, 16)

            def load_mask(b):
                if b >= MR:
                    pool.wait_ge(S["smx"], 2 * (b - MR + 1))
                gather(mask[:, b % MR, :], masks, im[:, b:b + 1], mask_sem[b % MR])

            nc.gpsimd.memset(w0bd[:, :, :], 0.0).then_inc(S["w0z"], 1)
            nc.gpsimd.memset(w2bd[:, :, :], 0.0).then_inc(S["w2z"], 1)
            pool.wait_ge(S["it"], 1)
            for g in (2, 0, 1):
                n = GR[g]
                gather(tb[0:n, g:g + 1], table, it[0:n, g:g + 1], S["tab"])
            pool.wait_ge(S["tab"], 16 * NG)
            for g in (2, 0, 1):
                n = GR[g]
                gather(win[0:n, g, :], kv, tb[0:n, g:g + 1], win_sem[g])
            pool.wait_ge(S["im"], 1)
            for b in range(MR):
                load_mask(b)
            pool.wait_ge(S["idx"], 1)
            pool.wait_ge(S["pre"], 16)
            for i in range(NT):
                pool.wait_ge(S["kve"], i + 1)
                pool.wait_ge(S["rot"], i // HT + 1)
                pool.indirect_dma_start(
                    out=kv_new.rearrange("u (o c) -> (u o) c", o=BLOCK),
                    out_offset=bass.IndirectOffsetOnAxis(ap=isc[:, i:i + 1], axis=0),
                    in_=kvn[:, i, :], in_offset=None,
                    bounds_check=NU * BLOCK - 1, oob_is_err=False).then_inc(sc_sem, 16)
            pool.wait_ge(sc_sem, 16 * NT)
            for g in range(NG):
                n = GR[g]
                gather(win[0:n, g, :], kv_new, iov[0:n, g:g + 1], ov_sem[g], bounds_check=NU - 1, oob_is_err=False)
            for b in range(MR, B):
                load_mask(b)

        def kv_evac(eng, kind, n, copy):
            g, o4 = n // (BLOCK // 4), n % (BLOCK // 4)
            ns = GR[g] // B
            eng.wait_ge(S["vtp" if kind else "ktp"], n + 1)
            src = ps[(4 if kind else 6) + n % 2][:, 0:4 * GR[g]].rearrange("p (o s b) -> p o s b", o=4, b=B)
            dst = (VT if kind else KT)[:, :, 4 * g:4 * g + ns, 4 * o4:4 * o4 + 4].rearrange("p b s o -> p o s b")
            for k in range(4):
                last = copy(dst[:, k], src[:, k])
            last.then_inc(S["vte" if kind else "kte"], 1)

        def acopy(dst, src):
            return nc.scalar.activation(dst, src, ACT.Copy)

        NQ = NG * BLOCK // 4

        def part(n):
            return ((H, G), (H, G), (0, H), (0, H))[n] + (n % 2,)

        @block.scalar
        def _(act):
            act.dma_start(fd[:, :], fdata).then_inc(S["fdata"], 16)
            act.dma_start(wqkv_sb[:, :, :], wqkv).then_inc(S["wqkv"], 16)
            act.dma_start(wo_sb[:, :, :], wo).then_inc(S["wo"], 16)
            act.dma_start(w3_sb[:, :, :], w3).then_inc(S["w3"], 16)
            act.dma_start(ball_sb[:, :], ball).then_inc(S["ball"], 16)
            act.wait_ge(S["trig"], 1)
            nc.scalar.activation(sinT[:, :, :], sinT[:, :, :], ACT.Sin).then_inc(S["sin"], 1)
            nc.scalar.activation(cosT[:, :, :], cosT[:, :, :], ACT.Sin, bias=C("halfpi"), scale=-1.0)\
                .then_inc(S["sin"], 1)

            def tile_out(i):
                act.wait_ge(S["x0p"], i + 1)
                if i >= 2:
                    act.wait_ge(S["qkvp"], i - 1)
                acopy(x0T[:, i % 2, :, :].rearrange("p a b -> p (a b)"), ps[i % 2][:, 0:256]).then_inc(S["x0s"], 1)

            def qkv_out(i):
                act.wait_ge(S["qkvp"], i + 1)
                acopy(qk[:, i, :], ps[2 + i % 2][:, 0:384]).then_inc(S["qke"], 1)
                acopy(kvn[:, i, G * HD:], ps[2 + i % 2][:, 384:512]).then_inc(S["kve"], 1)

            def squares(n):
                h0, nh, half = part(n)
                act.wait_ge(S["qke"], HT * (half + 1))
                if n >= 1:
                    act.wait_ge(S["rot"], n)
                nc.scalar.activation(sq[:, :, 0:nh * HD], qk[:, HT * half:HT * half + HT, h0 * HD:(h0 + nh) * HD],
                                     ACT.Square).then_inc(S["sqs"], 1)

            def root(n):
                _h, nh, _half = part(n)
                act.wait_ge(S["ss"], n + 1)
                nc.scalar.activation(st[:, 1, 0:nh * HT], st[:, 0, 0:nh * HT], ACT.Sqrt).then_inc(S["rt"], 1)

            tile_out(0)
            for i in range(NT):
                if i + 1 < NT:
                    tile_out(i + 1)
                qkv_out(i)
                if i == HT - 1:
                    squares(0)
                    root(0)
            for n in range(1, 4):
                squares(n)
                root(n)
            for n in range(NQ):
                kv_evac(act, 0, n, acopy)
            for n in range(STEPS):
                if (i := tail_tile(n, 2)) is not None:
                    act.wait_ge(S["x1p"], i + 1)
                    acopy(x1[:, i % 2, :], ps[PS_X][:, 0:256]).then_inc(S["x1e"], 1)
                if (i := tail_tile(n, 5)) is not None:
                    act.wait_ge(S["yp"], i + 1)
                    if i >= 2:
                        act.wait_ge(out_sem[i % 2], 16 * (i // 2))
                    acopy(res[:, i % 2, :], ps[PS_Y][:, 0:256]).then_inc(S["ye"], 1)
                m = n - LAG_P
                if 0 <= m < B:
                    act.wait_ge(S["ptp"], m + 1)
                    if m >= 2:
                        act.wait_ge(S["ob"], m - 1)
                    acopy(PT[:, m % 2, :, :, :].rearrange("p a b c -> p (a b c)"), ps[PS_P[m % 2]][0:HP, :])\
                        .then_inc(S["pte"], 1)
                if n < B:
                    act.wait_ge(S["nm"], n + 1)
                    if n >= PR:
                        act.wait_ge(S["ptp"], n - PR + 1)
                    for p in range(2):
                        nc.scalar.activation(pr[:, n % PR, p, :], sm[:, n % 2, p, :], ACT.Exp,
                                             bias=nmx[:, n, p:p + 1], scale=SCALE,
                                             accum_out=ssum[:, n, p:p + 1]).then_inc(S["ex"], 1)

        @block.vector
        def _(dve):
            chain = [0]

            def link(ins):
                chain[0] += 1
                ins.then_inc(S["dch"], 1)
                dve.wait_ge(S["dch"], chain[0])

            v = nc.vector
            dve.wait_ge(S["ints"], 16)
            dve.wait_ge(S["consts"], 16)
            v.tensor_scalar(ia[:, 0, :], ii[:, 0:NPOS], 4, None, ALU.arith_shift_right)
            link(v.tensor_scalar(ia[:, 1, :], ii[:, 0:NPOS], 15, None, ALU.bitwise_and))
            link(v.tensor_copy(fa[:, :, :], ia[:, :, :]))
            slot_row = fa[:, 0, NT:NT + 1]
            slot_b, off_b = fa[:, 0, NT + 1:NPOS], fa[:, 1, NT + 1:NPOS]
            off_tok = fa[:, 1, 0:NT]
            link(v.tensor_scalar(fr[:, 0, :], C("s8"), slot_row, 0.0, ALU.add, ALU.max))
            v.tensor_scalar(it[:, :], fr[:, 0, :], float(NBLK - 1), C("b257"), ALU.min, ALU.add)\
                .then_inc(S["it"], 1)
            ang, red = cosT, SS[:, :, 0, :]
            link(v.tensor_scalar(tk[:, 0, :], I("kvtok"), C("t"), None, ALU.add))
            link(v.tensor_tensor(ang[:, :, :], tk[:, 0, :].unsqueeze(2).broadcast_to([P, NT, 16]),
                                 C("invf").unsqueeze(1).broadcast_to([P, NT, 16]), ALU.mult))
            turns = CC[:, :, 0, :]
            link(v.tensor_scalar(turns, ang[:, :, :], 1.0 / 6.283185307179586, MAGIC, ALU.mult, ALU.add))
            link(v.tensor_scalar(turns, turns, MAGIC, None, ALU.subtract))
            src = ang[:, :, :]
            for piece in TWO_PI:
                link(v.scalar_tensor_tensor(out=red, in0=turns, scalar=-piece, in1=src,
                                            op0=ALU.mult, op1=ALU.add))
                src = red
            link(v.tensor_scalar(red, red, PI, -PI, ALU.min, ALU.max))
            v.tensor_copy(sinT[:, :, :], red)
            v.scalar_tensor_tensor(out=cosT[:, :, :], in0=red, scalar=-1.0, in1=red,
                                   op0=ALU.mult, op1=ALU.max).then_inc(S["trig"], 1)
            link(v.tensor_scalar(imf[:, :], slot_b, float(NMASK - 1), float(NA), ALU.min, ALU.mult))
            v.scalar_tensor_tensor(out=im[:, :], in0=off_b, scalar=C("t"), in1=imf[:, :],
                                   op0=ALU.add, op1=ALU.add).then_inc(S["im"], 1)
            link(v.tensor_scalar(tk[:, 1, :], off_tok, C("t"), None, ALU.add))
            v.tensor_scalar(tk[:, 2, :], tk[:, 1, :], 15.5, None, ALU.is_gt)
            link(v.tensor_scalar(tk[:, 3, :], tk[:, 1, :], 31.5, None, ALU.is_gt))
            link(v.tensor_tensor(tk[:, 4, :], tk[:, 2, :], tk[:, 3, :], ALU.add))
            link(v.scalar_tensor_tensor(out=tk[:, 4, :], in0=tk[:, 4, :], scalar=-16.0, in1=tk[:, 1, :],
                                        op0=ALU.mult, op1=ALU.add))
            link(v.tensor_tensor(tj[:, :].rearrange("p (k b) -> p k b", k=NW),
                                 C("j0").rearrange("p (k b) -> p k b", k=NW),
                                 off_b.unsqueeze(1).broadcast_to([P, NW, B]), ALU.subtract))

            def u_row(a, n=NT, m=NU):
                return a.unsqueeze(1).broadcast_to([P, n, m])

            def u_col(a, n=NT, m=NU):
                return a.unsqueeze(2).broadcast_to([P, n, m])

            off_row, o_col = u_row(off_b, NT, B), u_col(tk[:, 4, :], NT, B)
            link(v.tensor_tensor(m_b[:, :, :], u_row(tj[:, :]), u_col(tk[:, 4, :]), ALU.add))
            v.tensor_tensor(m_c[:, :, 0:B], o_col, off_row, ALU.is_ge)
            link(v.tensor_tensor(m_c[:, :, 2 * B:NU], o_col, off_row, ALU.is_lt))
            v.tensor_tensor(m_b[:, :, 0:B], m_b[:, :, 0:B], m_c[:, :, 0:B], ALU.mult)
            link(v.tensor_tensor(m_b[:, :, 2 * B:NU], m_b[:, :, 2 * B:NU], m_c[:, :, 2 * B:NU], ALU.mult))
            dve.wait_ge(S["fdata"], 16)
            link(v.tensor_scalar(sc1[:, :, :].rearrange("p a b -> p (a b)"), fd[:, 0:64], 1.0, None, ALU.add))
            v.tensor_scalar(m3[:, :], I("adapt"), C("aid"), fd[:, 64:65], ALU.is_equal, ALU.mult)
            dve.wait_ge(S["sin"], 2)
            for dst, src in ((CC, cosT), (SS, sinT)):
                ins = v.tensor_tensor(dst[:, :, :, :], src[:, :, :].unsqueeze(2).broadcast_to([P, NT, 4, 16]),
                                      sc1[:, :, :].unsqueeze(1).broadcast_to([P, NT, 4, 16]), ALU.mult)
            link(ins)

            def mixing(wbd, sems, i, name):
                dve.wait_ge(sems[i], 16 * BPT)
                v.tensor_tensor(wbd[:, i, :], wbd[:, i, :], ident, ALU.add).then_inc(S[name], 1)

            dve.wait_ge(S["tab"], 16 * NG)
            v.tensor_copy(rep[:, 0, :], tb[0:NU, 2:3].broadcast_to([NU, P])).then_inc(S["rep"], 1)
            v.tensor_copy(tbf[:, 0:2], tb[:, 0:2])
            link(v.tensor_copy(tbf[0:NU, 2:3], tb[0:NU, 2:3]))
            mixing(w0bd, w0_sem, 0, "w0bd")
            mixing(w0bd, w0_sem, 1, "w0bd")
            dve.wait_ge(S["repp"], 1)
            link(v.tensor_copy(wr[:, 0, :], ps[7][:, 0:NU]))
            link(v.memset(m_a[:, 0:NG, :], 0.0))
            v.tensor_tensor(m_a[:, 0:2, :], u_row(wr[:, 0, :], 2), u_col(tbf[:, 0:2], 2), ALU.is_equal)
            link(v.tensor_tensor(m_a[0:NU, 2, :], wr[0:NU, 0, :], tbf[0:NU, 2:3].broadcast_to([NU, NU]),
                                 ALU.is_equal))
            link(v.tensor_tensor(m_a[:, 0:NG, :], m_a[:, 0:NG, :], u_row(C("u1"), NG), ALU.mult))
            link(v.tensor_reduce(fr[:, 1, :], m_a[:, 0:NG, :], AX_X, ALU.max))
            v.tensor_copy(rep[:, 1, :], fr[0:NU, 1, 2:3].broadcast_to([NU, P])).then_inc(S["rep"], 1)
            link(v.tensor_scalar(fr[:, 2, :], fr[:, 1, :], 0.5, 4096.0, ALU.is_lt, ALU.mult))
            link(v.scalar_tensor_tensor(out=iov[:, :], in0=fr[:, 1, :], scalar=-1.0, in1=fr[:, 2, :],
                                        op0=ALU.add, op1=ALU.add))
            mixing(w0bd, w0_sem, 2, "w0bd")
            dve.wait_ge(S["repp"], 2)
            link(v.tensor_copy(wr[:, 1, :], ps[7][:, 128:128 + NU]))
            for j in range(BPT):
                q = slice(32 * j, 32 * j + 32)
                ins = v.tensor_copy(wt[q, :, :, :],
                                    wr[q, :, :].rearrange("p a (k i j) -> p a k i j", k=NW, j=BPT)[:, :, :, :, j])
            link(ins)
            v.tensor_tensor(tw[:, 0, :, :], wt[:, :, 1, :], wt[:, :, 0, :], ALU.subtract)
            link(v.tensor_tensor(tw[:, 1, :, :], wt[:, :, 2, :], wt[:, :, 1, :], ALU.subtract))
            v.tensor_tensor(tw[:, 0, :, :], tw[:, 0, :, :], u_row(tk[:, 2, :], 2, NT), ALU.mult)
            link(v.tensor_tensor(tw[:, 1, :, :], tw[:, 1, :, :], u_row(tk[:, 3, :], 2, NT), ALU.mult))
            link(v.tensor_tensor(tw[:, 0, :, :], tw[:, 0, :, :], tw[:, 1, :, :], ALU.add))
            link(v.tensor_tensor(tw[:, 0, :, :], tw[:, 0, :, :], wt[:, :, 0, :], ALU.add))
            blk_tok, rep_tok = tw[:, 0, 0, :], tw[:, 0, 1, :]
            link(v.tensor_tensor(m_a[:, :, :], u_row(wr[:, 0, :]), u_col(blk_tok), ALU.is_equal))
            link(v.tensor_tensor(m_b[:, :, :], m_b[:, :, :], m_a[:, :, :], ALU.mult))
            link(v.tensor_reduce(tk[:, 5, :], m_b[:, :, :], AX_X, ALU.max))
            link(v.tensor_tensor(tk[:, 6, :], tk[:, 5, :], C("j1"), ALU.is_gt))
            link(v.scalar_tensor_tensor(out=tk[:, 7, :], in0=rep_tok, scalar=float(BLOCK), in1=tk[:, 4, :],
                                        op0=ALU.mult, op1=ALU.add))
            link(v.scalar_tensor_tensor(out=tk[:, 7, :], in0=tk[:, 6, :], scalar=65536.0, in1=tk[:, 7, :],
                                        op0=ALU.mult, op1=ALU.add))
            v.tensor_scalar(isc[:, :], tk[:, 7, :], -float(BLOCK), None, ALU.add).then_inc(S["idx"], 1)
            for i in range(3, NT):
                mixing(w0bd, w0_sem, i, "w0bd")

            def rope(n):
                h0, nh, half = part(n)
                w = nh * HD
                tiles = slice(HT * half, HT * half + HT)
                s = [st[:, k, 0:nh * HT] for k in range(8)]
                dve.wait_ge(S["sqs"], n + 1)
                link(v.tensor_reduce(s[2].rearrange("p (i h) -> p i h", h=nh),
                                     sq[:, :, 0:w].rearrange("p i (h d) -> p i h d", d=HD), AX_X, ALU.add))
                v.tensor_scalar(s[0], s[2], 1.0 / HD, EPS, ALU.mult, ALU.add).then_inc(S["ss"], 1)
                dve.wait_ge(S["rt"], n + 1)
                link(v.reciprocal(s[3], s[1]))
                link(v.tensor_tensor(s[4], s[3], s[3], ALU.mult))
                link(v.tensor_tensor(s[5], s[4], s[0], ALU.mult))
                link(v.tensor_scalar(s[6], s[5], -0.5, 1.5, ALU.mult, ALU.add))
                link(v.tensor_tensor(s[7], s[3], s[6], ALU.mult))
                a = 0 if h0 == 0 else 2

                def heads(t):
                    return t.rearrange("p i (h d) -> p i h d", d=HD)

                def table(t):
                    return t[:, tiles, a:a + 2, :].rearrange("p i a d -> p i (a d)").unsqueeze(2)\
                        .broadcast_to([P, HT, nh, HD])

                raw = heads(qk[:, tiles, h0 * HD:h0 * HD + w])
                y, tc, tsn = heads(yn[:, :, 0:w]), heads(sq[:, :, 0:w]), heads(ts_[:, :, 0:w])
                link(v.tensor_tensor(y, raw, s[7].rearrange("p (i h) -> p i h", h=nh).unsqueeze(3)
                                     .broadcast_to([P, HT, nh, HD]), ALU.mult))
                v.tensor_tensor(tc, y, table(CC), ALU.mult)
                link(v.tensor_tensor(tsn, y, table(SS), ALU.mult))
                dst = raw if h0 == 0 else heads(kvn[:, tiles, 0:G * HD])
                v.tensor_tensor(dst[:, :, :, 0:16], tc[:, :, :, 0:16], tsn[:, :, :, 16:32], ALU.subtract)
                link_rot = v.tensor_tensor(dst[:, :, :, 16:32], tc[:, :, :, 16:32], tsn[:, :, :, 0:16], ALU.add)
                link_rot.then_inc(S["rot"], 1)

            def q_out(i):
                dve.wait_ge(S["qtp"], i + 1)
                v.tensor_copy(qT[:, BPT * i:BPT * i + BPT, :, :].rearrange("p b h t -> p h b t"),
                              ps[i % 2][:, 0:256].rearrange("p (h b t) -> p h b t", h=HPG, b=BPT))\
                    .then_inc(S["qte"], 1)

            for n in range(4):
                rope(n)
            dve.wait_ge(S["w3"], 16)
            for c in range(2):
                v.tensor_tensor(w3_sb[:, c, c * P:(c + 1) * P], w3_sb[:, c, c * P:(c + 1) * P], ident, ALU.add)\
                    .then_inc(S["w3i"], 1)
            for i in range(NT):
                q_out(i)
            for i in range(NT):
                mixing(w2bd, w2_sem, i, "w2bd")
            for n in range(NQ):
                kv_evac(dve, 1, n, v.tensor_copy)

            for n in range(STEPS):
                if (i := tail_tile(n, 1)) is not None:
                    dve.wait_ge(S["ob"], BPT * (i + 1))
                    v.tensor_copy(oT[:, i % 2, :, :].rearrange("p h (b t) -> p b h t", b=BPT),
                                  ps[PS_O][:, 0:256].rearrange("p (b h t) -> p b h t", b=BPT, h=HPG))\
                        .then_inc(S["oe"], 1)
                if (i := tail_tile(n, 3)) is not None:
                    dve.wait_ge(S["x2p"], i + 1)
                    v.tensor_copy(x2T[:, i % 2, :, :].rearrange("p a b -> p (a b)"), ps[PS_X][:, 256:512])\
                        .then_inc(S["x2e"], 1)
                if (i := tail_tile(n, 4)) is not None:
                    dve.wait_ge(S["xap"], i + 1)
                    v.tensor_tensor(xaT[:, i % 2, :].rearrange("p (b t) -> p b t", b=BPT),
                                    ps[PS_X][:, 0:P].rearrange("p (b t) -> p b t", b=BPT),
                                    m3[:, BPT * i:BPT * i + BPT].unsqueeze(2).broadcast_to([P, BPT, T]),
                                    ALU.mult).then_inc(S["xae"], 1)
                if n < B:
                    dve.wait_ge(S["scp"], n + 1)
                    dve.wait_ge(mask_sem[n % MR], 16 * (n // MR + 1))
                    if n >= 2:
                        dve.wait_ge(S["ex"], 2 * (n - 1))
                    for p in range(2):
                        v.tensor_tensor_reduce(
                            out=sm[:, n % 2, p, :], in0=ps[PS_S[p]][:, 0:SP_], in1=mask[:, n % MR, :],
                            scale=1.0, scalar=-3e38, op0=ALU.add, op1=ALU.max, accum_out=mx[:, n, p:p + 1])\
                            .then_inc(S["smx"], 1)
                    dve.wait_ge(S["smx"], 2 * (n + 1))
                    v.tensor_scalar(nmx[:, n, :], mx[:, n, :], -SCALE, None, ALU.mult).then_inc(S["nm"], 1)
                m = n - 1
                if 0 <= m < B:
                    dve.wait_ge(S["ex"], 2 * (m + 1))
                    v.reciprocal(rs[:, m, :], ssum[:, m, :]).then_inc(S["rc"], 1)
                    dve.wait_ge(S["rc"], m + 1)
                    v.tensor_tensor(pr[:, m % PR, :, :], pr[:, m % PR, :, :],
                                    rs[:, m, :].unsqueeze(2).broadcast_to([P, 2, SP_]), ALU.mult)\
                        .then_inc(S["pn"], 1)
                if n < B and n % 2 == 0:
                    dve.wait_ge(S["vtp"], NQ + n // 2 + 1)
                    if n >= 2 * BPT:
                        dve.wait_ge(S["ob"], n - 2 * BPT + 2)
                    v.tensor_copy(V[:, (n // BPT) % 2, n % BPT:n % BPT + 2, :, :].rearrange("p a b c -> p (a b c)"),
                                  ps[PS_V][0:HP, :]).then_inc(S["vte"], 1)

        @block.tensor
        def _(pe):
            mm = nc.tensor.matmul
            pe.wait_ge(S["consts"], 16)

            def replicate(k):
                pe.wait_ge(S["rep"], k + 1)
                mm(ps[7][:, 128 * k:128 * k + NU], rep[:, k, :], ident[0:NU, 0:NU], start=True, stop=True)\
                    .then_inc(S["repp"], 1)

            replicate(0)
            pe.wait_ge(S["x"], 16)

            def x0(i):
                pe.wait_ge(S["w0bd"], i + 1)
                if i >= 2:
                    pe.wait_ge(S["x0s"], i - 1)
                for c in range(2):
                    last = mm(ps[i % 2][:, c * P:(c + 1) * P], xs[:, i, c * P:(c + 1) * P], w0bd[:, i, :],
                              start=True, stop=True)
                last.then_inc(S["x0p"], 1)

            x0(0)
            for i in range(NT):
                if i + 1 < NT:
                    x0(i + 1)
                pe.wait_ge(S["x0s"], i + 1)
                if i == 0:
                    pe.wait_ge(S["wqkv"], 16)
                if i >= 2:
                    pe.wait_ge(S["kve"], i - 1)
                for c in range(2):
                    last = mm(ps[2 + i % 2][:, :], x0T[:, i % 2, c, :], wqkv_sb[:, c, :], start=(c == 0),
                              stop=(c == 1))
                last.then_inc(S["qkvp"], 1)
                if i == 0:
                    replicate(1)
            pe.wait_ge(S["x0s"], NT)
            for i in range(NT):
                pe.wait_ge(S["rot"], 3 + i // HT)
                if i >= 2:
                    pe.wait_ge(S["qte"], i - 1)
                for h in range(HPG):
                    last = nc.tensor.transpose(ps[i % 2][:, h * P:(h + 1) * P], qk[:, i, h * P:(h + 1) * P], ident)
                last.then_inc(S["qtp"], 1)

            n = 0
            for g in range(NG):
                m = GR[g]
                pe.wait_ge(ov_sem[g], 16)
                for o4 in range(BLOCK // 4):
                    for kind in range(2):
                        if n >= 2:
                            pe.wait_ge(S["vte" if kind else "kte"], n - 1)
                        for k in range(4):
                            a = (4 * o4 + k) * KVW + kind * P
                            last = nc.tensor.transpose(ps[(4 if kind else 6) + n % 2][:, k * m:(k + 1) * m],
                                                       win[0:m, g, a:a + P], ident[0:m, 0:m])
                        last.then_inc(S["vtp" if kind else "ktp"], 1)
                    n += 1
            pe.wait_ge(S["kte"], NQ)
            pe.wait_ge(S["vte"], NQ)
            pe.wait_ge(S["qte"], NT)

            def scores(b):
                if b >= 1:
                    pe.wait_ge(S["smx"], 2 * b)
                for g in range(G):
                    rows = slice(32 * g, 32 * g + 32)
                    last = mm(ps[PS_S[g // 2]][64 * (g % 2):64 * (g % 2) + 64, 0:SP_],
                              qT[rows, b, :, :].rearrange("p h t -> p (h t)"),
                              KT[rows, b, :, :].rearrange("p s o -> p (s o)"), start=True, stop=True)
                last.then_inc(S["scp"], 1)

            def values(b):
                if b >= 2:
                    pe.wait_ge(S["vte"], NQ + b // 2)
                for k in range(4):
                    bb, c = b + k // 2, k % 2
                    last = nc.tensor.transpose(
                        ps[PS_V][0:HP, k * P:(k + 1) * P],
                        VT[:, bb, :, :].rearrange("p s o -> p (s o)")[:, c * HP:(c + 1) * HP], ident)
                last.then_inc(S["vtp"], 1)

            def p_transpose(b):
                pe.wait_ge(S["pn"], b + 1)
                if b >= 2:
                    pe.wait_ge(S["pte"], b - 1)
                for c in range(2):
                    for p in range(2):
                        last = nc.tensor.transpose(ps[PS_P[b % 2]][0:HP, (2 * c + p) * P:(2 * c + p + 1) * P],
                                                   pr[:, b % PR, p, c * HP:(c + 1) * HP], ident)
                last.then_inc(S["ptp"], 1)

            def pv(b):
                pe.wait_ge(S["pte"], b + 1)
                pe.wait_ge(S["vte"], NQ + b // 2 + 1)
                j = b % BPT
                if j == 0 and b >= BPT:
                    pe.wait_ge(S["oe"], b // BPT)
                for g in range(G):
                    for c in range(2):
                        last = mm(ps[PS_O][32 * g:32 * g + 32, 64 * j:64 * j + 64],
                                  V[:, (b // BPT) % 2, j, c, 32 * g:32 * g + 32],
                                  PT[:, b % 2, c, g // 2, 64 * (g % 2):64 * (g % 2) + 64],
                                  start=(c == 0), stop=(c == 1))
                last.then_inc(S["ob"], 1)

            def tail_x1(i):
                if i == 0:
                    pe.wait_ge(S["wo"], 16)
                pe.wait_ge(S["oe"], i + 1)
                if i >= 1:
                    pe.wait_ge(S["xae"], i)
                mm(ps[PS_X][:, 0:256], w0bd[:, i, :], xs[:, i, :], start=True, stop=False)
                for h in range(HPG):
                    last = mm(ps[PS_X][:, 0:256], oT[:, i % 2, h, :], wo_sb[:, h, :], start=False,
                              stop=(h == HPG - 1))
                last.then_inc(S["x1p"], 1)

            def tail_x2(i):
                pe.wait_ge(S["x1e"], i + 1)
                pe.wait_ge(S["w2bd"], i + 1)
                for c in range(2):
                    last = mm(ps[PS_X][:, 256 + c * P:256 + (c + 1) * P], x1[:, i % 2, c * P:(c + 1) * P],
                              w2bd[:, i, :], start=True, stop=True)
                last.then_inc(S["x2p"], 1)

            def tail_xa(i):
                if i == 0:
                    pe.wait_ge(S["w3i"], 2)
                pe.wait_ge(S["x2e"], i + 1)
                for c in range(2):
                    last = mm(ps[PS_X][:, 0:P], w3_sb[:, c, 256:384], x2T[:, i % 2, c, :], start=(c == 0),
                              stop=(c == 1))
                last.then_inc(S["xap"], 1)
                if i >= 1:
                    pe.wait_ge(S["ye"], i)
                for c in range(2):
                    mm(ps[PS_Y][:, 0:256], x2T[:, i % 2, c, :], w3_sb[:, c, 0:256], start=(c == 0), stop=False)

            def tail_y(i):
                if i == 0:
                    pe.wait_ge(S["ball"], 16)
                pe.wait_ge(S["xae"], i + 1)
                mm(ps[PS_Y][:, 0:256], xaT[:, i % 2, :], ball_sb[:, :], start=False, stop=True)\
                    .then_inc(S["yp"], 1)

            for n in range(STEPS):
                if n < B:
                    scores(n)
                if 0 <= n - LAG_P < B:
                    p_transpose(n - LAG_P)
                if n < B and n % 2 == 0:
                    values(n)
                for stage, tail in ((1, tail_x1), (2, tail_x2), (3, tail_xa), (4, tail_y)):
                    if (i := tail_tile(n, stage)) is not None:
                        tail(i)
                if 0 <= n - LAG_O < B:
                    pv(n - LAG_O)


def _constants(np):
    p = np.arange(P)
    c = np.zeros((P, NC_), np.float32)

    def put(name, a):
        o, w = C_AT[name]
        c[:, o:o + w] = a

    put("ident", np.eye(P))
    u = np.arange(NU)
    put("u1", u + 1)
    put("j0", T * (u % B) + BLOCK * (u // B) + 1)
    half = HD // 2
    put("invf", np.float32(1.0) / np.float32(10000.0) ** (np.arange(half, dtype=np.float32) / np.float32(half)))
    put("s8", BPT * np.arange(NG)[None, :] + (p // B)[:, None] - WINDOW // BLOCK)
    put("b257", (p % B * NBLK)[:, None])
    put("t", (p % T)[:, None])
    put("j1", P * np.arange(NT)[None, :] + p[:, None] + 1)
    put("aid", (p // 16)[:, None])
    put("halfpi", np.pi / 2)
    put("eps", EPS)
    return c


def _masks(np):
    s, a, rel = np.ogrid[0:NMASK, 0:NA, 0:SP_]
    seen = (rel > a) & (rel <= a + WINDOW) & (rel >= WINDOW - BLOCK * s)
    return np.where(seen, 0.0, -BIG).astype(np.float32).reshape(NMASK * NA, SP_)


def kernel(**inputs):
    import numpy as np
    import concourse.bacc as bacc
    from concourse.bass_utils import run_bass_kernel_spmd as run

    a = {k: np.asarray(v) for k, v in inputs.items()}

    def tok(v):
        return np.repeat(v.reshape(NT, BPT).T, T, axis=0)

    def row(v):
        return np.broadcast_to(v[None, :], (P, B))

    kvl = a["itok_B_37_3939"].astype(np.int32)
    ints = np.concatenate([tok(kvl), np.tile(kvl, BPT)[:, None], row(kvl), row(a["itok_B_0_7"].astype(np.int32)),
                           row(a["itok_B_1_198"].astype(np.int32)), row(a["itok_B_0_6"].astype(np.int32))], axis=1)
    kvc = np.empty((NPHYS, BLOCK, 2, G, HD), np.float32)
    kvc[:, :, 0] = a["L1_cond_k_blocks"].transpose(0, 2, 1, 3)
    kvc[:, :, 1] = a["L1_cond_v_blocks"].transpose(0, 2, 1, 3)
    fdata = np.concatenate([np.broadcast_to(a["L1_cond_q_norm_scale"][None, :], (P, HD)),
                            np.broadcast_to(a["L1_cond_k_norm_scale"][None, :], (P, HD)),
                            np.repeat(a["L3_cond_scalings"], 16)[:, None]], axis=1)

    def split(w):
        return w.reshape(2, P, -1).transpose(1, 0, 2)

    wq = a["L1_cond_Wq"].reshape(G, HPG, HD, D).transpose(1, 0, 2, 3).reshape(H * HD, D)
    wqkv = split(np.concatenate([wq, a["L1_cond_Wk"], a["L1_cond_Wv"]], axis=0).T)
    wo = a["L1_cond_Wo"].T.reshape(G, HPG, HD, D).transpose(0, 2, 1, 3).reshape(P, HPG, D)
    w3 = split(np.concatenate([a["L3_cond_W"].T, a["L3_cond_A"].reshape(P, D).T], axis=1))
    arrays = {
        "x": a["x"].reshape(B * T, D), "ints": ints, "consts": _constants(np), "fdata": fdata,
        "table": a["itok_Bx257_0_4111"].astype(np.int32).reshape(B * NBLK, 1),
        "kv": kvc.reshape(NPHYS, BLOCK * KVW),
        "w0": a["L0_cond_weights"], "w2": a["L2_cond_weights"], "masks": _masks(np),
        "wqkv": wqkv, "wo": wo, "w3": w3,
        "ball": a["L3_cond_Bm"].transpose(0, 2, 1).reshape(P, D),
    }
    arrays = {k: np.ascontiguousarray(v) for k, v in arrays.items()}
    nc = bacc.Bacc("TRN2", target_bir_lowering=False, num_devices=1)
    aps = {k: nc.dram_tensor(k, v.shape, mybir.dt.from_np(v.dtype), kind="ExternalInput").ap()
           for k, v in arrays.items()}
    out = nc.dram_tensor("out", (B * T, D), F32, kind="ExternalOutput").ap()
    program(nc, aps["x"], aps["ints"], aps["consts"], aps["fdata"], aps["table"], aps["masks"], aps["kv"], aps["w0"], aps["w2"],
            aps["wqkv"], aps["wo"], aps["w3"], aps["ball"], out)
    r = run(nc, [arrays], core_ids=[0])
    return np.asarray(r.results[0]["out"]).reshape(B, T, D)
```

```python
import concourse.bass as bass
from concourse import mybir
from contextlib import ExitStack

F32 = mybir.dt.float32
I32 = mybir.dt.int32
ALU = mybir.AluOpType
ACT = mybir.ActivationFunctionType
AX_X = mybir.AxisListType.X

P = 128
B, T, D = 32, 32, 256
G, HPG, HD = 4, 2, 32
H = G * HPG
BLOCK, NBLK, NPHYS = 16, 257, 4112
WINDOW = 128
SCALE = 256.0 ** -0.5
EPS = 1e-6
NT = B * T // P
BPT = P // T
NS = WINDOW // BLOCK + 3
NW = 3
SP_ = NS * BLOCK
CH = (96, 80)
NU = NW * B
GB = 8
NG = B // GB
PG = 12 * GB
NR = NS * GB
NO = (NS - NW) * GB
KVW = 2 * G * HD
BIG = 1e30
PI = 3.1415925
TWO_PI = (6.28125, 0.0019350051879882812, 3.019916050561733e-07)
MAGIC = 12582912.0

_C = [("ident", 128), ("ones", 128), ("u1", NU), ("j0", NU), ("invf", 16), ("s8", NG + 1), ("b257", NG + 1),
      ("own", NG), ("t", 1), ("j1", NT), ("aid", 1), ("halfpi", 1)]
C_AT, NC_ = {}, 0
for _n, _w in _C:
    C_AT[_n] = (NC_, _w)
    NC_ += _w
_I = [("kvtok", NT), ("kvrow", NG + 1), ("kvb", B), ("subj", NT), ("cond", NT), ("adapt", B), ("row", NT)]
I_AT, NI_ = {}, 0
for _n, _w in _I:
    I_AT[_n] = (NI_, _w)
    NI_ += _w
NPOS = NT + NG + 1 + B
NMASK = WINDOW // BLOCK + 1
NA = BLOCK - 1 + T
HT = NT // 2
MR = 12
PR = 3




def program(nc, x, ints, consts, fdata, table, masks, kv, w0, w2, wqkv, wo, w3, ball, out):
    kv_new = nc.dram_tensor("kv_new", (NU, BLOCK * KVW), F32, kind="Internal").ap()
    v_win = nc.dram_tensor("v_win", (NG, NS, BLOCK, GB, P), F32, kind="Internal").ap()
    x_rows = x.rearrange("(i p) f -> p i f", p=P)
    out_rows = out.rearrange("(i p) f -> p i f", p=P)

    ctx = ExitStack()
    with ctx:
        def sb(name, shape, dt=F32):
            return ctx.enter_context(nc.sbuf_tensor(name, shape, dt))

        def pb(name, shape, dt=F32):
            return ctx.enter_context(nc.psum_tensor(name, shape, dt))

        def sem(name):
            return ctx.enter_context(nc.semaphore(name))

        cst = sb("cst", [P, NC_])
        ii = sb("ii", [P, NI_], I32)
        fd = sb("fd", [P, 65])
        xs = sb("xs", [P, NT, D])
        wqkv_sb = sb("wqkv_sb", [P, 2, 512])
        wo_sb = sb("wo_sb", [P, HPG, D])
        w3_sb = sb("w3_sb", [P, 2, 384])
        ball_sb = sb("ball_sb", [P, D])
        win = sb("win", [PG, NG, BLOCK * KVW])
        KT = sb("KT", [P, 2, GB, NS, BLOCK])
        qT = sb("qT", [P, B, HPG, T])
        mask = sb("mask", [P, MR, SP_])
        w0bd = sb("w0bd", [P, NT, P])
        w2bd = sb("w2bd", [P, NT, P])
        x0T = sb("x0T", [P, NT, 2, P])
        q = sb("q", [P, NT, H * HD])
        kvn = sb("kvn", [P, NT, KVW])
        sq = sb("sq", [P, HT, H * HD])
        yn = sb("yn", [P, HT, H * HD])
        tc_ = sb("tc_", [P, HT, H * HD])
        ts_ = sb("ts_", [P, HT, H * HD])
        st = sb("st", [P, 8, HT * H])
        cosT = sb("cosT", [P, NT, 16])
        sinT = sb("sinT", [P, NT, 16])
        sc1 = sb("sc1", [P, 4, 16])
        CC = sb("CC", [P, NT, 4, 16])
        SS = sb("SS", [P, NT, 4, 16])
        m3 = sb("m3", [P, B])
        ia = sb("ia", [P, 2, NPOS], I32)
        fa = sb("fa", [P, 2, NPOS])
        i0 = sb("i0", [P, NT], I32)
        i2 = sb("i2", [P, NT], I32)
        it = sb("it", [P, NG + 1], I32)
        fr = sb("fr", [P, 4, NG + 1])
        tb = sb("tb", [PG, NG + 1], I32)
        tbf = sb("tbf", [PG, NG + 1])
        tbk = sb("tbk", [PG, NG], I32)
        rep = sb("rep", [NU, 2, NU])
        wr = sb("wr", [P, 2, NU])
        wt = sb("wt", [P, 2, NW, NT])
        iov = sb("iov", [PG, NG], I32)
        isc = sb("isc", [P, NT], I32)
        im = sb("im", [P, B], I32)
        imf = sb("imf", [P, B])
        tk = sb("tk", [P, 8, NT])
        tw = sb("tw", [P, 2, 2, NT])
        tj = sb("tj", [P, NU])
        mx = sb("mx", [P, B, 2])
        nmx = sb("nmx", [P, B, 2])
        ssum = sb("ssum", [P, B, 2])
        rs = sb("rs", [P, B, 2])
        V = sb("V", [CH[0], 2, 2, GB, P])
        own = V[:, :, :, :, :].rearrange("p a c b f -> p (a c b f)")
        scratch = KT[:, :, :, :, :].rearrange("p a b s o -> p (a b s o)")
        m_a, m_b, m_c = (scratch[:, k * NT * NU:(k + 1) * NT * NU].rearrange("p (i u) -> p i u", u=NU)
                         for k in range(3))
        sm = sb("sm", [P, 2, 2, SP_])
        pr = sb("pr", [P, PR, 2, SP_])
        PT = sb("PT", [CH[0], 2, 2, 2, P])
        oT = sb("oT", [P, 2, HPG, P])
        x1 = sb("x1", [P, 2, D])
        x2T = sb("x2T", [P, 2, 2, P])
        xaT = sb("xaT", [P, 2, P])
        res = sb("res", [P, 2, D])

        def C(name):
            a, w = C_AT[name]
            return cst[:, a:a + w]

        def I(name):
            a, w = I_AT[name]
            return ii[:, a:a + w]

        ident = C("ident")

        ps = [pb(f"ps{i}", [P, 512]) for i in range(8)]
        PS_S, PS_P, PS_W, PS_Q, PS_O, PS_X, PS_Y = (0, 1), 2, 3, 4, 5, 6, 7

        names = ("ints consts fdata wqkv wo w3 ball tab pre it rep repp im tbz i0 i2 own tbk row cand pch trig sin idx "
                 "w0bd w2bd w3i x0p x0s kvp kve qp qe xtp xte sqs ss rt inv rot qtp qte wp we wev vst "
                 "scp smx nm ex rc pn ptp pte ob oe x1p x1e x2p x2e xap xae yp ye dch").split()
        S = {n: sem("s_" + n) for n in names}
        win_sem = [sem(f"s_win_{i}") for i in range(NG)]
        w0_sem = [sem(f"s_w0_{i}") for i in range(NT)]
        w2_sem = [sem(f"s_w2_{i}") for i in range(NT)]
        ov_sem = [sem(f"s_ov_{i}") for i in range(NG)]
        v_sem = [sem(f"s_v_{i}") for i in range(NG)]
        x_sem = [sem(f"s_x_{i}") for i in range(2)]
        tabown = sem("s_tabown")
        mask_sem = [sem(f"s_mask_{i}") for i in range(MR)]
        sc_sem = sem("s_sc")
        out_sem = [sem(f"s_out_{i}") for i in range(2)]

        block = ctx.enter_context(nc.Block())

        LAG_P, LAG_O = 2, 3

        def tail_tile(n, stage):
            m = n - LAG_O - stage
            return m // BPT if m >= 0 and m % BPT == BPT - 1 and m < B else None

        STEPS = B + LAG_O + 6
        WF = BLOCK // 4

        def window_fill_at(n):
            first = 1 if n < GB else GB - WF
            f = (n // GB + 1) * WF + n % GB - first
            return f if first <= n % GB < first + WF and n < B and f < NG * WF else None

        def window_bank(f):
            return (PS_W, PS_Q, PS_X, PS_Y)[f] if f < WF else PS_W

        X_FIRST = 7
        X_AT = {2: (7,)}
        Q_AT = {2: ((4, PS_Q), (5, PS_X), (6, PS_Y), (7, PS_O))}

        def u_row(a, n=NT, m=NU):
            return a.unsqueeze(1).broadcast_to([P, n, m])

        def u_col(a, n=NT, m=NU):
            return a.unsqueeze(2).broadcast_to([P, n, m])

        off_b = fa[:, 1, NT + NG + 1:NPOS]

        def part(n):
            return (G if n < 2 else H), n % 2

        def rope_operands(n):
            nh, half = part(n)
            w, a = nh * HD, 2 if n < 2 else 0
            tiles = slice(HT * half, HT * half + HT)

            def heads(t):
                return t.rearrange("p i (h d) -> p i h d", d=HD)

            def table(t):
                return t[:, tiles, a:a + 2, :].rearrange("p i a d -> p i (a d)").unsqueeze(2)\
                    .broadcast_to([P, HT, nh, HD])

            return (heads((kvn if n < 2 else q)[:, tiles, 0:w]), heads(yn[:, :, 0:w]), heads(tc_[:, :, 0:w]),
                    heads(ts_[:, :, 0:w]), table(CC), table(SS),
                    st[:, 7, 0:nh * HT].rearrange("p (i h) -> p i h", h=nh).unsqueeze(3).broadcast_to([P, HT, nh, HD]))

        @block.sync
        def _(sp):
            sp.dma_start(ii[:, :], ints).then_inc(S["ints"], 16)
            sp.dma_start(cst[:, :], consts).then_inc(S["consts"], 16)
            for half in range(2):
                tiles = slice(HT * half, HT * half + HT)
                sp.dma_start(xs[:, tiles, :], x_rows[:, tiles, :]).then_inc(x_sem[half], 16)

            sp.wait_ge(S["own"], 16)
            sp.dma_start(kv_new, own).then_inc(S["pre"], 16)
            for g in range(NG):
                sp.wait_ge(ov_sem[g], 16)
                rows = win[:, g, :].rearrange("p (o c) -> p o c", c=KVW)[:, :, P:KVW]
                for s in range(NS):
                    sp.dma_start(v_win[g, s].rearrange("o b f -> b o f"), rows[GB * s:GB * s + GB])\
                        .then_inc(S["vst"], 16)
                sp.wait_ge(S["vst"], 16 * NS * (g + 1))
                if g >= 2:
                    sp.wait_ge(S["ob"], GB * (g - 1))
                v_rows = v_win[g].rearrange("s o b f -> (s o) (b f)")
                for c in range(2):
                    sp.dma_start(V[0:CH[c], g % 2, c, :, :].rearrange("p b f -> p (b f)"),
                                 v_rows[c * CH[0]:c * CH[0] + CH[c], :]).then_inc(v_sem[g], 16)

        @block.gpsimd
        def _(pool):
            def gather(dst, src, idx, s, **kw):
                pool.indirect_dma_start(out=dst, out_offset=None, in_=src,
                                        in_offset=bass.IndirectOffsetOnAxis(ap=idx, axis=0), **kw).then_inc(s, 16)

            def load_mask(b):
                if b >= MR:
                    pool.wait_ge(S["smx"], 2 * (b - MR + 1))
                gather(mask[:, b % MR, :], masks, im[:, b:b + 1], mask_sem[b % MR])

            def load_mix(wbd, w, idx, i, sems):
                gather(wbd[:, i, :], w, idx[:, i:i + 1], sems[i])

            def load_table(g):
                gather(tb[:, g:g + 1], table, it[0:PG, g:g + 1], tabown if g == NG else S["tab"],
                       bounds_check=B * NBLK - 1, oob_is_err=False)

            def load_window(g):
                gather(win[:, g, :], kv, tbk[:, g:g + 1], win_sem[g], bounds_check=NPHYS - 1, oob_is_err=False)

            placed = [0]

            def order(ins):
                placed[0] += 1
                ins.then_inc(S["pch"], 1)
                pool.wait_ge(S["pch"], placed[0])

            nc.gpsimd.memset(tb[:, :], 2 * NPHYS).then_inc(S["tbz"], 1)
            pool.wait_ge(S["i0"], 1)
            for i in range(2):
                load_mix(w0bd, w0, i0, i, w0_sem)
            pool.wait_ge(S["it"], 1)
            pool.wait_ge(S["tbz"], 1)
            load_table(NG)
            for i in range(2, 4):
                load_mix(w0bd, w0, i0, i, w0_sem)
            for g in range(NG):
                load_table(g)
            pool.wait_ge(tabown, 16)
            gather(own, kv, tb[:, NG:NG + 1], S["own"], bounds_check=NPHYS - 1, oob_is_err=False)
            for i in range(4, NT):
                load_mix(w0bd, w0, i0, i, w0_sem)
            pool.wait_ge(S["row"], 3)
            order(nc.gpsimd.tensor_tensor(tj[:, :].rearrange("p (k b) -> p k b", k=NW),
                                          C("j0").rearrange("p (k b) -> p k b", k=NW),
                                          off_b.unsqueeze(1).broadcast_to([P, NW, B]), ALU.subtract))
            order(nc.gpsimd.tensor_tensor(m_b[:, :, :], u_row(tj[:, :]), u_col(tk[:, 4, :]), ALU.add))
            nc.gpsimd.tensor_tensor(m_b[:, :, 0:B], m_b[:, :, 0:B], m_c[:, :, 0:B], ALU.mult)\
                .then_inc(S["cand"], 1)
            nc.gpsimd.tensor_tensor(m_b[:, :, 2 * B:NU], m_b[:, :, 2 * B:NU], m_c[:, :, 2 * B:NU], ALU.mult)\
                .then_inc(S["cand"], 1)
            pool.wait_ge(S["im"], 1)
            for b in range(2):
                load_mask(b)
            pool.wait_ge(S["tbk"], 1)
            load_window(0)
            for b in range(2, 4):
                load_mask(b)
            load_window(1)
            for b in range(4, 6):
                load_mask(b)
            pool.wait_ge(S["idx"], 1)
            pool.wait_ge(S["pre"], 16)
            for i in range(NT):
                pool.wait_ge(S["kve"], i + 1)
                pool.wait_ge(S["rot"], i // HT + 1)
                pool.indirect_dma_start(
                    out=kv_new.rearrange("u (o c) -> (u o) c", o=BLOCK),
                    out_offset=bass.IndirectOffsetOnAxis(ap=isc[:, i:i + 1], axis=0),
                    in_=kvn[:, i, :], in_offset=None,
                    bounds_check=NU * BLOCK - 1, oob_is_err=False).then_inc(sc_sem, 16)
            pool.wait_ge(sc_sem, 16 * NT)

            def residual_2(i):
                pool.wait_ge(w2_sem[i], 16)
                nc.gpsimd.tensor_tensor(w2bd[:, i, :], w2bd[:, i, :], ident, ALU.add).then_inc(S["w2bd"], 1)

            def overlay(g):
                pool.wait_ge(win_sem[g], 16)
                gather(win[:, g, :], kv_new, iov[:, g:g + 1], ov_sem[g], bounds_check=NU - 1, oob_is_err=False)

            overlay(0)
            overlay(1)
            pool.wait_ge(S["i2"], 1)
            raw, y, tc, tsn, cc, ss, inv = rope_operands(3)
            combine = nc.gpsimd.tensor_tensor
            pool.wait_ge(S["qe"], NT)
            pool.wait_ge(S["rot"], 3)
            combine(tc, raw, cc, ALU.mult)
            order(combine(tsn, raw, ss, ALU.mult))
            combine(y[:, :, :, 0:16], tc[:, :, :, 0:16], tsn[:, :, :, 16:32], ALU.subtract)
            order(combine(y[:, :, :, 16:32], tc[:, :, :, 16:32], tsn[:, :, :, 0:16], ALU.add))
            pool.wait_ge(S["inv"], 4)
            combine(raw, y, inv, ALU.mult).then_inc(S["rot"], 1)
            for b in range(6, MR):
                load_mask(b)
            for i in range(4):
                load_mix(w2bd, w2, i2, i, w2_sem)
            pool.wait_ge(v_sem[0], 32)
            load_window(2)
            load_window(3)
            for i in range(4):
                residual_2(i)
            load_mix(w2bd, w2, i2, 4, w2_sem)
            load_mix(w2bd, w2, i2, 5, w2_sem)
            overlay(2)
            for b in range(MR, MR + 4):
                load_mask(b)
            overlay(3)
            load_mix(w2bd, w2, i2, 6, w2_sem)
            load_mix(w2bd, w2, i2, 7, w2_sem)
            for b in range(MR + 4, MR + 6):
                load_mask(b)
            for i in range(4, NT):
                residual_2(i)
            for b in range(MR + 6, B):
                load_mask(b)

        def acopy(dst, src):
            return nc.scalar.activation(dst, src, ACT.Copy)

        def window_out(f, copy):
            g, o = f // WF, 4 * (f % WF)
            engine = nc.scalar if copy is acopy else nc.vector
            engine.wait_ge(S["wp"], f + 1)
            copy(KT[:, g % 2, :, :, o:o + 4].rearrange("p b s o -> p o s b"),
                 ps[window_bank(f)][:, 0:4 * NR].rearrange("p (o s b) -> p o s b", o=4, b=GB))\
                .then_inc(S["we" if copy is acopy else "wev"], 1)

        @block.scalar
        def _(act):
            act.dma_start(wqkv_sb[:, :, :], wqkv).then_inc(S["wqkv"], 16)
            act.dma_start(fd[:, :], fdata).then_inc(S["fdata"], 16)
            act.wait_ge(S["trig"], 1)
            nc.scalar.activation(sinT[:, :, :], sinT[:, :, :], ACT.Sin).then_inc(S["sin"], 1)
            nc.scalar.activation(cosT[:, :, :], cosT[:, :, :], ACT.Sin, bias=C("halfpi"), scale=-1.0)\
                .then_inc(S["sin"], 1)

            act.dma_start(wo_sb[:, :, :], wo).then_inc(S["wo"], 16)
            act.dma_start(w3_sb[:, :, :], w3).then_inc(S["w3"], 16)
            act.dma_start(ball_sb[:, :], ball).then_inc(S["ball"], 16)

            def x0T_out(i):
                act.wait_ge(S["x0p"], i + 1)
                acopy(x0T[:, i, :, :].rearrange("p a b -> p (a b)"), ps[i % 2][:, 0:256]).then_inc(S["x0s"], 1)

            def squares(n):
                nh, half = part(n)
                tiles = slice(HT * half, HT * half + HT)
                if n >= 1:
                    act.wait_ge(S["ss"], n)
                src = kvn if n < 2 else q
                act.wait_ge(S["kve" if n < 2 else "qe"], HT * (half + 1))
                nc.scalar.activation(sq[:, :, 0:nh * HD], src[:, tiles, 0:nh * HD], ACT.Square).then_inc(S["sqs"], 1)

            def root(n):
                nh, _half = part(n)
                act.wait_ge(S["ss"], n + 1)
                nc.scalar.activation(st[:, 1, 0:nh * HT], st[:, 0, 0:nh * HT], ACT.Sqrt).then_inc(S["rt"], 1)

            def q_raw(i):
                act.wait_ge(S["qp"], i + 1)
                acopy(q[:, i, :], ps[4 + i % 2][:, 0:256]).then_inc(S["qe"], 1)

            def x0_out(i):
                act.wait_ge(S["xtp"], i + 1)
                acopy(xs[:, i, :], ps[6 + i % 2][:, 0:256]).then_inc(S["xte"], 1)

            x0T_out(0)
            for i in range(NT):
                if i == HT:
                    x0T_out(i)
                if i + 1 not in (HT, NT):
                    x0T_out(i + 1)
                act.wait_ge(S["kvp"], i + 1)
                acopy(kvn[:, i, :], ps[2 + i % 2][:, 0:KVW]).then_inc(S["kve"], 1)
                if i == HT - 1:
                    squares(0)
                    root(0)
            squares(1)
            for i in range(HT):
                q_raw(i)
            root(1)
            squares(2)
            for i in range(HT, NT):
                q_raw(i)
            root(2)
            squares(3)
            for i in range(2):
                x0_out(i)
            root(3)
            for i in range(2, X_FIRST):
                x0_out(i)
            for f in (0, 1):
                window_out(f, acopy)
            for n in range(STEPS):
                if (i := tail_tile(n, 5)) is not None:
                    act.wait_ge(S["yp"], i + 1)
                    if i >= 2:
                        act.wait_ge(out_sem[i % 2], 16 * (i // 2))
                    acopy(res[:, i % 2, :], ps[PS_Y][:, 0:256]).then_inc(S["ye"], 1)
                    act.wait_ge(S["ye"], i + 1)
                    act.dma_start(out_rows[:, i, :], res[:, i % 2, :]).then_inc(out_sem[i % 2], 16)
                m = n - LAG_P
                if 0 <= m < B:
                    act.wait_ge(S["ptp"], m + 1)
                    if m >= 2:
                        act.wait_ge(S["ob"], m - 1)
                    for c in range(2):
                        last = acopy(PT[0:CH[c], m % 2, c, :, :].rearrange("p b c -> p (b c)"),
                                     ps[PS_P][0:CH[c], 256 * c:256 * c + 256])
                    last.then_inc(S["pte"], 1)
                for i in X_AT.get(n, ()):
                    x0_out(i)
                if (f := window_fill_at(n)) is not None:
                    window_out(f, acopy)
                if n < B:
                    act.wait_ge(S["nm"], n + 1)
                    if n >= PR:
                        act.wait_ge(S["ptp"], n - PR + 1)
                    for p in range(2):
                        nc.scalar.activation(pr[:, n % PR, p, :], sm[:, n % 2, p, :], ACT.Exp,
                                             bias=nmx[:, n, p:p + 1], scale=SCALE,
                                             accum_out=ssum[:, n, p:p + 1]).then_inc(S["ex"], 1)
            for j in range(2):
                act.wait_ge(out_sem[j], 16 * NT // 2)

        @block.vector
        def _(dve):
            chain = [0]

            def link(ins):
                chain[0] += 1
                ins.then_inc(S["dch"], 1)
                dve.wait_ge(S["dch"], chain[0])

            v = nc.vector
            dve.wait_ge(S["ints"], 16)
            v.scalar_tensor_tensor(out=i0[:, :], in0=I("subj"), scalar=float(P), in1=I("row"), op0=ALU.mult,
                                   op1=ALU.add).then_inc(S["i0"], 1)
            v.scalar_tensor_tensor(out=i2[:, :], in0=I("cond"), scalar=float(P), in1=I("row"), op0=ALU.mult,
                                   op1=ALU.add).then_inc(S["i2"], 1)
            v.tensor_scalar(ia[:, 0, :], ii[:, 0:NPOS], 4, None, ALU.arith_shift_right)
            link(v.tensor_scalar(ia[:, 1, :], ii[:, 0:NPOS], 15, None, ALU.bitwise_and))
            link(v.tensor_copy(fa[:, :, :], ia[:, :, :]))
            slot_row = fa[:, 0, NT:NT + NG + 1]
            slot_b = fa[:, 0, NT + NG + 1:NPOS]
            off_tok = fa[:, 1, 0:NT]
            dve.wait_ge(S["consts"], 16)
            link(v.tensor_tensor(fr[:, 0, :], slot_row, C("s8"), ALU.add))
            link(v.tensor_scalar(fr[:, 0, :], fr[:, 0, :], 0.0, float(NBLK - 1), ALU.max, ALU.min))
            v.tensor_tensor(it[:, :], fr[:, 0, :], C("b257"), ALU.add).then_inc(S["it"], 1)
            ang, red = cosT, SS[:, :, 0, :]
            link(v.tensor_scalar(tk[:, 0, :], I("kvtok"), C("t"), None, ALU.add))
            link(v.tensor_tensor(ang[:, :, :], tk[:, 0, :].unsqueeze(2).broadcast_to([P, NT, 16]),
                                 C("invf").unsqueeze(1).broadcast_to([P, NT, 16]), ALU.mult))
            turns = CC[:, :, 0, :]
            link(v.tensor_scalar(turns, ang[:, :, :], 1.0 / 6.283185307179586, MAGIC, ALU.mult, ALU.add))
            link(v.tensor_scalar(turns, turns, MAGIC, None, ALU.subtract))
            src = ang[:, :, :]
            for piece in TWO_PI:
                link(v.scalar_tensor_tensor(out=red, in0=turns, scalar=-piece, in1=src,
                                            op0=ALU.mult, op1=ALU.add))
                src = red
            link(v.tensor_scalar(red, red, PI, -PI, ALU.min, ALU.max))
            v.tensor_copy(sinT[:, :, :], red)
            v.scalar_tensor_tensor(out=cosT[:, :, :], in0=red, scalar=-1.0, in1=red,
                                   op0=ALU.mult, op1=ALU.max).then_inc(S["trig"], 1)
            link(v.tensor_scalar(imf[:, :], slot_b, float(NMASK - 1), float(NA), ALU.min, ALU.mult))
            v.scalar_tensor_tensor(out=im[:, :], in0=off_b, scalar=C("t"), in1=imf[:, :],
                                   op0=ALU.add, op1=ALU.add).then_inc(S["im"], 1)

            def mixing(i):
                dve.wait_ge(w0_sem[i], 16)
                v.tensor_tensor(w0bd[:, i, :], w0bd[:, i, :], ident, ALU.add).then_inc(S["w0bd"], 1)

            for i in range(HT):
                mixing(i)
            link(v.tensor_scalar(tk[:, 1, :], off_tok, C("t"), None, ALU.add))
            v.tensor_scalar(tk[:, 2, :], tk[:, 1, :], 15.5, None, ALU.is_gt)
            link(v.tensor_scalar(tk[:, 3, :], tk[:, 1, :], 31.5, None, ALU.is_gt))
            link(v.tensor_tensor(tk[:, 4, :], tk[:, 2, :], tk[:, 3, :], ALU.add))
            v.scalar_tensor_tensor(out=tk[:, 4, :], in0=tk[:, 4, :], scalar=-16.0, in1=tk[:, 1, :],
                                   op0=ALU.mult, op1=ALU.add).then_inc(S["row"], 1)
            dve.wait_ge(S["row"], 1)
            off_row, o_col = u_row(off_b, NT, B), u_col(tk[:, 4, :], NT, B)
            v.tensor_tensor(m_c[:, :, 0:B], o_col, off_row, ALU.is_ge).then_inc(S["row"], 1)
            v.tensor_tensor(m_c[:, :, 2 * B:NU], o_col, off_row, ALU.is_lt).then_inc(S["row"], 1)
            dve.wait_ge(S["fdata"], 16)
            link(v.tensor_scalar(sc1[:, :, :].rearrange("p a b -> p (a b)"), fd[:, 0:64], 1.0, None, ALU.add))
            v.tensor_scalar(m3[:, :], I("adapt"), C("aid"), fd[:, 64:65], ALU.is_equal, ALU.mult)
            dve.wait_ge(S["sin"], 2)
            for dst, src in ((CC, cosT), (SS, sinT)):
                ins = v.tensor_tensor(dst[:, :, :, :], src[:, :, :].unsqueeze(2).broadcast_to([P, NT, 4, 16]),
                                      sc1[:, :, :].unsqueeze(1).broadcast_to([P, NT, 4, 16]), ALU.mult)
            link(ins)

            def rope(n, stages=range(6)):
                raw, y, tc, tsn, cc, ss, inv = rope_operands(n)
                nh, _half = part(n)
                s = [st[:, k, 0:nh * HT] for k in range(8)]
                for stage in stages:
                    if stage == 0:
                        dve.wait_ge(S["sqs"], n + 1)
                        link(v.tensor_reduce(s[2].rearrange("p (i h) -> p i h", h=nh),
                                             sq[:, :, 0:nh * HD].rearrange("p i (h d) -> p i h d", d=HD), AX_X,
                                             ALU.add))
                        v.tensor_scalar(s[0], s[2], 1.0 / HD, EPS, ALU.mult, ALU.add).then_inc(S["ss"], 1)
                    elif stage == 1:
                        v.tensor_tensor(tc, raw, cc, ALU.mult)
                    elif stage == 2:
                        link(v.tensor_tensor(tsn, raw, ss, ALU.mult))
                    elif stage == 3:
                        v.tensor_tensor(y[:, :, :, 0:16], tc[:, :, :, 0:16], tsn[:, :, :, 16:32], ALU.subtract)
                        v.tensor_tensor(y[:, :, :, 16:32], tc[:, :, :, 16:32], tsn[:, :, :, 0:16], ALU.add)
                    elif stage == 4:
                        dve.wait_ge(S["rt"], n + 1)
                        link(v.reciprocal(s[3], s[1]))
                        link(v.tensor_tensor(s[4], s[3], s[3], ALU.mult))
                        link(v.tensor_tensor(s[5], s[4], s[0], ALU.mult))
                        link(v.tensor_scalar(s[6], s[5], -0.5, 1.5, ALU.mult, ALU.add))
                        v.tensor_tensor(s[7], s[3], s[6], ALU.mult).then_inc(S["inv"], 1)
                        if n < 3:
                            dve.wait_ge(S["inv"], n + 1)
                    else:
                        v.tensor_tensor(raw, y, inv, ALU.mult).then_inc(S["rot"], 1)

            def spread(k, src):
                v.tensor_scalar(rep[:, k, :], ident[0:NU, 0:NU], src, None, ALU.mult).then_inc(S["rep"], 1)

            def spread_out(k):
                dve.wait_ge(S["repp"], k + 1)
                link(v.tensor_copy(wr[:, k, :], ps[7][:, P * k:P * k + NU]))

            dve.wait_ge(tabown, 16)
            dve.wait_ge(S["tab"], 16 * NG)
            link(v.tensor_copy(tbf[:, :], tb[:, :]))
            v.tensor_tensor(tbk[:, :], tbf[:, 0:NG], C("own")[0:PG], ALU.add).then_inc(S["tbk"], 1)
            spread(0, tbf[:, NG:NG + 1])
            spread_out(0)
            link(v.tensor_tensor(m_a[0:PG, 0:NG + 1, :], u_row(wr[:, 0, :], NG + 1)[0:PG], tbf[:, :].unsqueeze(2)
                                 .broadcast_to([PG, NG + 1, NU]), ALU.is_equal))
            link(v.tensor_tensor(m_a[0:PG, 0:NG + 1, :], m_a[0:PG, 0:NG + 1, :], u_row(C("u1"), NG + 1)[0:PG],
                                 ALU.mult))
            link(v.tensor_reduce(fr[0:PG, 1, :], m_a[0:PG, 0:NG + 1, :], AX_X, ALU.max))
            spread(1, fr[0:PG, 1, NG:NG + 1])
            link(v.tensor_scalar(fr[0:PG, 2, :], fr[0:PG, 1, :], 0.5, 4096.0, ALU.is_lt, ALU.mult))
            v.scalar_tensor_tensor(out=iov[:, :], in0=fr[0:PG, 1, 0:NG], scalar=-1.0, in1=fr[0:PG, 2, 0:NG],
                                   op0=ALU.add, op1=ALU.add)
            rope(0, range(1))
            for i in range(HT, NT):
                mixing(i)
            rope(0, range(1, 6))
            spread_out(1)
            for j in range(BPT):
                quarter = slice(32 * j, 32 * j + 32)
                ins = v.tensor_copy(wt[quarter, :, :, :],
                                    wr[quarter, :, :].rearrange("p a (k i j) -> p a k i j", k=NW, j=BPT)[:, :, :, :, j])
            link(ins)
            v.tensor_tensor(tw[:, 0, :, :], wt[:, :, 1, :], wt[:, :, 0, :], ALU.subtract)
            link(v.tensor_tensor(tw[:, 1, :, :], wt[:, :, 2, :], wt[:, :, 1, :], ALU.subtract))
            v.tensor_tensor(tw[:, 0, :, :], tw[:, 0, :, :], u_row(tk[:, 2, :], 2, NT), ALU.mult)
            link(v.tensor_tensor(tw[:, 1, :, :], tw[:, 1, :, :], u_row(tk[:, 3, :], 2, NT), ALU.mult))
            link(v.tensor_tensor(tw[:, 0, :, :], tw[:, 0, :, :], tw[:, 1, :, :], ALU.add))
            link(v.tensor_tensor(tw[:, 0, :, :], tw[:, 0, :, :], wt[:, :, 0, :], ALU.add))
            blk_tok, rep_tok = tw[:, 0, 0, :], tw[:, 0, 1, :]
            dve.wait_ge(S["cand"], 2)
            link(v.tensor_tensor(m_a[:, :, :], u_row(wr[:, 0, :]), u_col(blk_tok), ALU.is_equal))
            link(v.tensor_tensor(m_b[:, :, :], m_b[:, :, :], m_a[:, :, :], ALU.mult))
            link(v.tensor_reduce(tk[:, 5, :], m_b[:, :, :], AX_X, ALU.max))
            link(v.tensor_tensor(tk[:, 6, :], tk[:, 5, :], C("j1"), ALU.is_gt))
            link(v.scalar_tensor_tensor(out=tk[:, 7, :], in0=rep_tok, scalar=float(BLOCK), in1=tk[:, 4, :],
                                        op0=ALU.mult, op1=ALU.add))
            link(v.scalar_tensor_tensor(out=tk[:, 7, :], in0=tk[:, 6, :], scalar=65536.0, in1=tk[:, 7, :],
                                        op0=ALU.mult, op1=ALU.add))
            v.tensor_scalar(isc[:, :], tk[:, 7, :], -float(BLOCK), None, ALU.add).then_inc(S["idx"], 1)

            def q_out(i, bank):
                dve.wait_ge(S["qtp"], i + 1)
                v.tensor_copy(qT[:, BPT * i:BPT * i + BPT, :, :].rearrange("p b h t -> p h b t"),
                              ps[bank][:, 0:256].rearrange("p (h b t) -> p h b t", h=HPG, b=BPT))\
                    .then_inc(S["qte"], 1)

            for n in range(1, 3):
                rope(n)
            for i in range(HT):
                q_out(i, i % 2)
            rope(3, (0, 4))
            for f in (2, 3):
                window_out(f, v.tensor_copy)
            dve.wait_ge(S["w3"], 16)
            for c in range(2):
                v.tensor_tensor(w3_sb[:, c, c * P:(c + 1) * P], w3_sb[:, c, c * P:(c + 1) * P], ident, ALU.add)\
                    .then_inc(S["w3i"], 1)

            for n in range(STEPS):
                if (i := tail_tile(n, 1)) is not None:
                    dve.wait_ge(S["ob"], BPT * (i + 1))
                    v.tensor_copy(oT[:, i % 2, :, :].rearrange("p h (b t) -> p b h t", b=BPT),
                                  ps[PS_O][:, 0:256].rearrange("p (b h t) -> p b h t", b=BPT, h=HPG))\
                        .then_inc(S["oe"], 1)
                if (i := tail_tile(n, 2)) is not None:
                    dve.wait_ge(S["x1p"], i + 1)
                    v.tensor_tensor(x1[:, i % 2, :], ps[PS_X][:, 0:256], xs[:, i, :], ALU.add).then_inc(S["x1e"], 1)
                if (i := tail_tile(n, 3)) is not None:
                    dve.wait_ge(S["x2p"], i + 1)
                    v.tensor_copy(x2T[:, i % 2, :, :].rearrange("p a b -> p (a b)"), ps[PS_X][:, 256:512])\
                        .then_inc(S["x2e"], 1)
                if (i := tail_tile(n, 4)) is not None:
                    dve.wait_ge(S["xap"], i + 1)
                    v.tensor_tensor(xaT[:, i % 2, :].rearrange("p (b t) -> p b t", b=BPT),
                                    ps[PS_X][:, 0:P].rearrange("p (b t) -> p b t", b=BPT),
                                    m3[:, BPT * i:BPT * i + BPT].unsqueeze(2).broadcast_to([P, BPT, T]),
                                    ALU.mult).then_inc(S["xae"], 1)
                if n < B:
                    dve.wait_ge(S["scp"], n + 1)
                    dve.wait_ge(mask_sem[n % MR], 16 * (n // MR + 1))
                    if n >= 2:
                        dve.wait_ge(S["ex"], 2 * (n - 1))
                    for p in range(2):
                        v.tensor_tensor_reduce(
                            out=sm[:, n % 2, p, :], in0=ps[PS_S[p]][:, 0:SP_], in1=mask[:, n % MR, :],
                            scale=1.0, scalar=-3e38, op0=ALU.add, op1=ALU.max, accum_out=mx[:, n, p:p + 1])\
                            .then_inc(S["smx"], 1)
                    dve.wait_ge(S["smx"], 2 * (n + 1))
                    v.tensor_scalar(nmx[:, n, :], mx[:, n, :], -SCALE, None, ALU.mult).then_inc(S["nm"], 1)
                m = n - 1
                if 0 <= m < B:
                    dve.wait_ge(S["ex"], 2 * (m + 1))
                    v.reciprocal(rs[:, m, :], ssum[:, m, :]).then_inc(S["rc"], 1)
                    dve.wait_ge(S["rc"], m + 1)
                    v.tensor_tensor(pr[:, m % PR, :, :], pr[:, m % PR, :, :],
                                    rs[:, m, :].unsqueeze(2).broadcast_to([P, 2, SP_]), ALU.mult)\
                        .then_inc(S["pn"], 1)
                for i, bank in Q_AT.get(n, ()):
                    q_out(i, bank)

        @block.tensor
        def _(pe):
            mm = nc.tensor.matmul
            pe.wait_ge(S["consts"], 16)

            def replicate(k):
                pe.wait_ge(S["rep"], k + 1)
                mm(ps[7][:, P * k:P * k + NU], C("ones")[0:NU, :], rep[:, k, :], start=True, stop=True)\
                    .then_inc(S["repp"], 1)

            def x0(i):
                if i % HT == 0:
                    pe.wait_ge(x_sem[i // HT], 16)
                pe.wait_ge(S["w0bd"], i + 1)
                if i >= 2:
                    pe.wait_ge(S["x0s"], i - 1)
                for c in range(2):
                    last = mm(ps[i % 2][:, c * P:(c + 1) * P], xs[:, i, c * P:(c + 1) * P], w0bd[:, i, :],
                              start=True, stop=True)
                last.then_inc(S["x0p"], 1)

            def project(i, bank, cols, done):
                for c in range(2):
                    last = mm(ps[bank][:, 0:256], x0T[:, i, c, :], wqkv_sb[:, c, cols:cols + 256], start=(c == 0),
                              stop=(c == 1))
                last.then_inc(S[done], 1)

            x0(0)
            pe.wait_ge(S["wqkv"], 16)
            for i in range(NT):
                if i == HT:
                    x0(i)
                if i + 1 not in (HT, NT):
                    x0(i + 1)
                pe.wait_ge(S["x0s"], i + 1)
                if i >= 2:
                    pe.wait_ge(S["kve"], i - 1)
                project(i, 2 + i % 2, 256, "kvp")
                if i == 1:
                    replicate(0)
                if i == HT - 1:
                    replicate(1)
            for i in range(NT):
                if i >= 2:
                    pe.wait_ge(S["qe"], i - 1)
                project(i, 4 + i % 2, 0, "qp")

            def q_transpose(i, bank):
                pe.wait_ge(S["rot"], 3 + i // HT)
                if i == HT:
                    pe.wait_ge(S["xte"], NT)
                for h in range(HPG):
                    last = nc.tensor.transpose(ps[bank][:, h * P:(h + 1) * P], q[:, i, h * P:(h + 1) * P], ident)
                last.then_inc(S["qtp"], 1)

            for i in range(HT):
                if i >= 2:
                    pe.wait_ge(S["qte"], i - 1)
                q_transpose(i, i % 2)

            def residual(i):
                if i == 1:
                    pe.wait_ge(S["idx"], 1)
                if i >= 2:
                    pe.wait_ge(S["xte"], i - 1)
                mm(ps[6 + i % 2][:, 0:256], w0bd[:, i, :], xs[:, i, :], start=True, stop=True).then_inc(S["xtp"], 1)

            for i in range(X_FIRST):
                residual(i)

            def window_fill(f):
                g, o = f // WF, 4 * (f % WF)
                if f % WF == 0:
                    pe.wait_ge(ov_sem[g], 16)
                if f in (2, 3):
                    pe.wait_ge(S["xte"], X_FIRST)
                if f >= WF:
                    pe.wait_ge(S["we"], max(1, f - 2))
                for k in range(4):
                    last = nc.tensor.transpose(ps[window_bank(f)][:, k * NR:(k + 1) * NR],
                                               win[0:NR, g, (o + k) * KVW:(o + k) * KVW + P], ident[0:NR, 0:NR])
                last.then_inc(S["wp"], 1)

            pe.wait_ge(S["qe"], NT)
            for f in range(WF):
                window_fill(f)
            pe.wait_ge(S["qte"], HT)

            def scores(b):
                if b % GB == 0:
                    pe.wait_ge(S["we"], WF * (b // GB + 1) - 2)
                    if b == 0:
                        pe.wait_ge(S["wev"], 2)
                if b == BPT * HT:
                    pe.wait_ge(S["qte"], NT)
                if b >= 1:
                    pe.wait_ge(S["smx"], 2 * b)
                for g in range(G):
                    rows = slice(32 * g, 32 * g + 32)
                    last = mm(ps[PS_S[g // 2]][64 * (g % 2):64 * (g % 2) + 64, 0:SP_],
                              qT[rows, b, :, :].rearrange("p h t -> p (h t)"),
                              KT[rows, b // GB % 2, b % GB, :, :].rearrange("p s o -> p (s o)"), start=True, stop=True)
                last.then_inc(S["scp"], 1)

            def p_transpose(b):
                pe.wait_ge(S["pn"], b + 1)
                if b >= 1:
                    pe.wait_ge(S["pte"], b)
                for c in range(2):
                    for p in range(2):
                        last = nc.tensor.transpose(ps[PS_P][0:CH[c], (2 * c + p) * P:(2 * c + p + 1) * P],
                                                   pr[:, b % PR, p, c * CH[0]:c * CH[0] + CH[c]], ident)
                last.then_inc(S["ptp"], 1)

            def pv(b):
                pe.wait_ge(S["pte"], b + 1)
                if b % GB == 0:
                    pe.wait_ge(v_sem[b // GB], 32)
                j = b % BPT
                if b == 0:
                    pe.wait_ge(S["qte"], NT)
                elif j == 0:
                    pe.wait_ge(S["oe"], b // BPT)
                for g in range(G):
                    for c in range(2):
                        last = mm(ps[PS_O][32 * g:32 * g + 32, 64 * j:64 * j + 64],
                                  V[0:CH[c], b // GB % 2, c, b % GB, 32 * g:32 * g + 32],
                                  PT[0:CH[c], b % 2, c, g // 2, 64 * (g % 2):64 * (g % 2) + 64],
                                  start=(c == 0), stop=(c == 1))
                last.then_inc(S["ob"], 1)

            def tail_x1(i):
                if i == 0:
                    pe.wait_ge(S["wo"], 16)
                pe.wait_ge(S["oe"], i + 1)
                if i >= 1:
                    pe.wait_ge(S["xae"], i)
                for h in range(HPG):
                    last = mm(ps[PS_X][:, 0:256], oT[:, i % 2, h, :], wo_sb[:, h, :], start=(h == 0),
                              stop=(h == HPG - 1))
                last.then_inc(S["x1p"], 1)

            def tail_x2(i):
                pe.wait_ge(S["x1e"], i + 1)
                pe.wait_ge(S["w2bd"], i + 1)
                for c in range(2):
                    last = mm(ps[PS_X][:, 256 + c * P:256 + (c + 1) * P], x1[:, i % 2, c * P:(c + 1) * P],
                              w2bd[:, i, :], start=True, stop=True)
                last.then_inc(S["x2p"], 1)

            def tail_xa(i):
                if i == 0:
                    pe.wait_ge(S["w3i"], 2)
                pe.wait_ge(S["x2e"], i + 1)
                for c in range(2):
                    last = mm(ps[PS_X][:, 0:P], w3_sb[:, c, 256:384], x2T[:, i % 2, c, :], start=(c == 0),
                              stop=(c == 1))
                last.then_inc(S["xap"], 1)
                if i >= 1:
                    pe.wait_ge(S["ye"], i)
                for c in range(2):
                    mm(ps[PS_Y][:, 0:256], x2T[:, i % 2, c, :], w3_sb[:, c, 0:256], start=(c == 0), stop=False)

            def tail_y(i):
                if i == 0:
                    pe.wait_ge(S["ball"], 16)
                pe.wait_ge(S["xae"], i + 1)
                mm(ps[PS_Y][:, 0:256], xaT[:, i % 2, :], ball_sb[:, :], start=False, stop=True)\
                    .then_inc(S["yp"], 1)

            for n in range(STEPS):
                if n < B:
                    scores(n)
                if 0 <= n - LAG_P < B:
                    p_transpose(n - LAG_P)
                for i in X_AT.get(n, ()):
                    residual(i)
                if (f := window_fill_at(n)) is not None:
                    window_fill(f)
                for i, bank in Q_AT.get(n, ()):
                    q_transpose(i, bank)
                for stage, tail in ((1, tail_x1), (2, tail_x2), (3, tail_xa), (4, tail_y)):
                    if (i := tail_tile(n, stage)) is not None:
                        tail(i)
                if 0 <= n - LAG_O < B:
                    pv(n - LAG_O)


def _constants(np):
    p = np.arange(P)
    c = np.zeros((P, NC_), np.float32)

    def put(name, a):
        o, w = C_AT[name]
        c[:, o:o + w] = a

    put("ident", np.eye(P))
    u = np.arange(NU)
    put("ones", 1.0)
    put("u1", u + 1)
    put("j0", T * (u % B) + BLOCK * (u // B) + 1)
    half = HD // 2
    put("invf", np.float32(1.0) / np.float32(10000.0) ** (np.arange(half, dtype=np.float32) / np.float32(half)))
    slot = np.repeat((p // GB)[:, None], NG + 1, axis=1)
    slot[:, NG] = NS - NW + p // B
    batch = GB * np.arange(NG + 1)[None, :] + (p % GB)[:, None]
    batch[:, NG] = p % B
    put("s8", slot - WINDOW // BLOCK)
    put("b257", NBLK * batch + 65536 * (slot >= NS))
    put("own", 2 * NPHYS * ((p >= NO) & (p < NR))[:, None])
    put("t", (p % T)[:, None])
    put("j1", P * np.arange(NT)[None, :] + p[:, None] + 1)
    put("aid", (p // 16)[:, None])
    put("halfpi", np.pi / 2)
    return c


def _masks(np):
    s, a, rel = np.ogrid[0:NMASK, 0:NA, 0:SP_]
    seen = (rel > a) & (rel <= a + WINDOW) & (rel >= WINDOW - BLOCK * s)
    return np.where(seen, 0.0, -BIG).astype(np.float32).reshape(NMASK * NA, SP_)


def kernel(**inputs):
    import numpy as np
    import concourse.bacc as bacc
    from concourse.bass_utils import run_bass_kernel_spmd as run

    a = {k: np.asarray(v) for k, v in inputs.items()}

    def tok(v):
        return np.repeat(v.reshape(NT, BPT).T, T, axis=0)

    def row(v):
        return np.broadcast_to(v[None, :], (P, B))

    kvl = a["itok_B_37_3939"].astype(np.int32)
    ints = np.concatenate([tok(kvl), np.tile(kvl.reshape(NG, GB).T, (P // GB, 1)),
                           np.tile(kvl, BPT)[:, None], row(kvl),
                           tok(a["itok_B_0_7"].astype(np.int32)),
                           tok(a["itok_B_1_198"].astype(np.int32)), row(a["itok_B_0_6"].astype(np.int32)),
                           np.repeat(np.arange(P, dtype=np.int32)[:, None], NT, axis=1)], axis=1)
    kvc = np.empty((NPHYS, BLOCK, 2, G, HD), np.float32)
    kvc[:, :, 0] = a["L1_cond_k_blocks"].transpose(0, 2, 1, 3)
    kvc[:, :, 1] = a["L1_cond_v_blocks"].transpose(0, 2, 1, 3)
    fdata = np.concatenate([np.broadcast_to(a["L1_cond_q_norm_scale"][None, :], (P, HD)),
                            np.broadcast_to(a["L1_cond_k_norm_scale"][None, :], (P, HD)),
                            np.repeat(a["L3_cond_scalings"], 16)[:, None]], axis=1)

    def blocks(w):
        wide = np.zeros((w.shape[0], BPT, HD, BPT, HD), np.float32)
        for j in range(BPT):
            wide[:, j, :, j, :] = w
        return wide.reshape(-1, P)


    def split(w):
        return w.reshape(2, P, -1).transpose(1, 0, 2)

    wq = a["L1_cond_Wq"].reshape(G, HPG, HD, D).transpose(1, 0, 2, 3).reshape(H * HD, D)
    wqkv = split(np.concatenate([wq, a["L1_cond_Wk"], a["L1_cond_Wv"]], axis=0).T)
    wo = a["L1_cond_Wo"].T.reshape(G, HPG, HD, D).transpose(0, 2, 1, 3).reshape(P, HPG, D)
    w3 = split(np.concatenate([a["L3_cond_W"].T, a["L3_cond_A"].reshape(P, D).T], axis=1))
    arrays = {
        "x": a["x"].reshape(B * T, D), "ints": ints, "consts": _constants(np), "fdata": fdata,
        "table": a["itok_Bx257_0_4111"].astype(np.int32).reshape(B * NBLK, 1),
        "kv": kvc.reshape(NPHYS, BLOCK * KVW),
        "w0": blocks(a["L0_cond_weights"]), "w2": blocks(a["L2_cond_weights"]), "masks": _masks(np),
        "wqkv": wqkv, "wo": wo, "w3": w3,
        "ball": a["L3_cond_Bm"].transpose(0, 2, 1).reshape(P, D),
    }
    arrays = {k: np.ascontiguousarray(v) for k, v in arrays.items()}
    nc = bacc.Bacc("TRN2", target_bir_lowering=False, num_devices=1)
    aps = {k: nc.dram_tensor(k, v.shape, mybir.dt.from_np(v.dtype), kind="ExternalInput").ap()
           for k, v in arrays.items()}
    out = nc.dram_tensor("out", (B * T, D), F32, kind="ExternalOutput").ap()
    program(nc, aps["x"], aps["ints"], aps["consts"], aps["fdata"], aps["table"], aps["masks"], aps["kv"],
            aps["w0"], aps["w2"], aps["wqkv"], aps["wo"], aps["w3"], aps["ball"], out)
    r = run(nc, [arrays], core_ids=[0])
    return np.asarray(r.results[0]["out"]).reshape(B, T, D)
```
